# Optimizing a Trainium2 kernel written in Bass

```python
import numpy as np
import jax
import jax.numpy as jnp

def _softmax(x, axis=-1):
    return jax.nn.softmax(x, axis=axis)
def _gelu(x):
    return jax.nn.gelu(x, approximate=True)
def _silu(x):
    return jax.nn.silu(x)
def _sigmoid(x):
    return jax.nn.sigmoid(x)
def _layernorm(x, axis=-1, eps=1e-5):
    m = jnp.mean(x, axis=axis, keepdims=True)
    v = jnp.var(x, axis=axis, keepdims=True)
    return (x - m) / jnp.sqrt(v + eps)
def _scatter_add(tgt, idx, src, axis=0):
    return tgt.at[idx].add(src)
def _segment_sum(src, seg, n):
    return jax.ops.segment_sum(src, seg, n)

kernel_name = 'mk_conv_seq_d1_conv_nchw512_026e51'

def setup_inputs(seed: int = 0):
    np.random.seed(seed)
    _w = jnp.asarray
    def _rec_inputs():
        import jax
        import jax.numpy as jnp
        _gk = jax.random.key(seed)
        x = -0.000125 + 0.9999 * jax.random.normal(jax.random.fold_in(_gk, 1), (16, 512, 64, 64), jnp.float32)
        return x
    x = _rec_inputs()
    def _L0_conv_setup():
        import jax, jax.numpy as jnp
        import numpy as np
        B, C, H, W = (16, 512, 64, 64)
        CQ = C // 8
        NEG_INF = -1e+30
        key = jax.random.key(seed)
        ks = jax.random.split(key, 8)
        x = jax.random.normal(ks[0], (B, C, H, W), dtype=jnp.float32)
        Wq = jax.random.normal(ks[1], (CQ, C), dtype=jnp.float32) * 0.02
        bq = jnp.zeros((CQ,), dtype=jnp.float32)
        Wk = jax.random.normal(ks[2], (CQ, C), dtype=jnp.float32) * 0.02
        bk = jnp.zeros((CQ,), dtype=jnp.float32)
        Wv = jax.random.normal(ks[3], (C, C), dtype=jnp.float32) * 0.02
        bv = jnp.zeros((C,), dtype=jnp.float32)
        gamma = jnp.array([0.5], dtype=jnp.float32)
        return {'x': x, 'Wq': Wq, 'bq': bq, 'Wk': Wk, 'bk': bk, 'Wv': Wv, 'bv': bv, 'gamma': gamma}
    _L0_conv_all = _L0_conv_setup()
    _L0_conv_in = {k: v for k, v in _L0_conv_all.items() if k in ('Wq', 'bq', 'Wk', 'bk', 'Wv', 'bv', 'gamma', )}
    del _L0_conv_all

    return {
        "x": x,
        "L0_conv_Wq": _L0_conv_in["Wq"],
        "L0_conv_bq": _L0_conv_in["bq"],
        "L0_conv_Wk": _L0_conv_in["Wk"],
        "L0_conv_bk": _L0_conv_in["bk"],
        "L0_conv_Wv": _L0_conv_in["Wv"],
        "L0_conv_bv": _L0_conv_in["bv"],
        "L0_conv_gamma": _L0_conv_in["gamma"],
    }

def reference(x, L0_conv_Wq, L0_conv_bq, L0_conv_Wk, L0_conv_bk, L0_conv_Wv, L0_conv_bv, L0_conv_gamma):
    import jax
    import jax.numpy as jnp
    def _L0_conv_ref(x, Wq, bq, Wk, bk, Wv, bv, gamma):
        import jax, jax.numpy as jnp
        import numpy as np
        B, C, H, W = (16, 512, 64, 64)
        CQ = C // 8
        NEG_INF = -1e+30
        h = x.shape[2]
        q = jnp.einsum('bchw,oc->bohw', x, Wq) + bq[None, :, None, None]
        k = jnp.einsum('bchw,oc->bohw', x, Wk) + bk[None, :, None, None]
        v = jnp.einsum('bchw,oc->bohw', x, Wv) + bv[None, :, None, None]
        e_h = jnp.einsum('bchw,bcgw->bhwg', q, k)
        diag = jnp.eye(h, dtype=bool)[:, None, :]
        e_h = jnp.where(diag, NEG_INF, e_h)
        e_w = jnp.einsum('bchw,bchu->bhwu', q, k)
        att = jax.nn.softmax(jnp.concatenate([e_h, e_w], axis=3), axis=3)
        att_h = att[..., :h]
        att_w = att[..., h:]
        out_h = jnp.einsum('bcgw,bhwg->bchw', v, att_h)
        out_w = jnp.einsum('bchu,bhwu->bchw', v, att_w)
        return gamma[0] * (out_h + out_w) + x

    def _gn(v, G=32, eps=1e-5):
        B_, C_, H_, W_ = v.shape
        g = v.reshape(B_, G, C_ // G, H_, W_)
        m = jnp.mean(g, axis=(2, 3, 4), keepdims=True)
        s = jnp.var(g, axis=(2, 3, 4), keepdims=True)
        return ((g - m) / jnp.sqrt(s + eps)).reshape(v.shape)

    def _ln_c(v, eps=1e-6):
        m = jnp.mean(v, axis=1, keepdims=True)
        s = jnp.var(v, axis=1, keepdims=True)
        return (v - m) / jnp.sqrt(s + eps)

    def _ln_t(v, eps=1e-5):
        m = jnp.mean(v, axis=-1, keepdims=True)
        s = jnp.var(v, axis=-1, keepdims=True)
        return (v - m) / jnp.sqrt(s + eps)

    def _to_tokens(v):
        B_, C_, H_, W_ = v.shape
        return v.reshape(B_, C_, H_ * W_).transpose(0, 2, 1)
    def _from_tokens(t, like):
        B_, C_, H_, W_ = like.shape
        return t.transpose(0, 2, 1).reshape(B_, C_, H_, W_)

    x = _L0_conv_ref(x, L0_conv_Wq, L0_conv_bq, L0_conv_Wk, L0_conv_bk, L0_conv_Wv, L0_conv_bv, L0_conv_gamma)
    return x


_drawn_inputs = setup_inputs


def setup_inputs(seed=0):
    import zlib

    import numpy as np

    out = dict(_drawn_inputs(seed))
    spreads = {'L0_conv_bq': (0.0, 0.461), 'L0_conv_bk': (0.0, 0.8), 'L0_conv_bv': (0.0, 0.1)}
    factors = {}
    for name, (base, spread) in spreads.items():
        noise = np.random.default_rng([zlib.crc32(name.encode()), seed]).standard_normal(out[name].shape)
        drawn = base * np.exp(spread * noise) if base else spread * noise
        out[name] = jnp.asarray(drawn.astype(out[name].dtype))
    for name, factor in factors.items():
        out[name] = (out[name] * factor).astype(out[name].dtype)
    return out
```

```python
from contextlib import ExitStack

import concourse.bass as bass
from concourse import mybir

ALU = mybir.AluOpType
ACT = mybir.ActivationFunctionType
F32 = mybir.dt.float32
F32R = mybir.dt.float32r
F16 = mybir.dt.float16
I32 = mybir.dt.int32
AX_X = mybir.AxisListType.X
RMAX = bass.bass_isa.ReduceOp.max

P = 128
NEG_INF = -1e30
P_SCALE = 2.0 ** 12
V_EXP = 14
MANT = 1 << 23


def criss_cross(nc, x, wqk_t, bqk, wv_t, wv, bv, gamma, out):
    B, C, H, W = x.shape
    CH = C // P
    CQ = wqk_t.shape[1] // 2
    HALF = H // 2
    PIX = H * W
    assert CQ == 64 and H == W == 64 and C == CH * P and bqk.shape[0] == P
    UNITS = 8
    ROWS = HALF // UNITS
    SPLITS = HALF // 2
    GROUPS = HALF // 4
    SET = 8
    SETS = HALF // SET
    APPLY = [("row", 0)] + [("col", g) for g in range(SETS)] + [("row", g) for g in range(1, SETS)]
    TILES = SET * len(APPLY)
    COL_FROM, COL_TO = 8, 8 + HALF
    LAG = 2
    EXP_AT = 3
    STATS = 12
    RING = 4
    PITCH = W + 2

    v_dram = nc.dram_tensor("v_dram", (H, PITCH, 2 * C), F16, kind="Internal").ap()

    with ExitStack() as ctx:
        def sb(name, shape, dt):
            return ctx.enter_context(nc.sbuf_tensor(name, shape, dt))

        def sem(name):
            return ctx.enter_context(nc.semaphore(name))

        xs = sb("xs", [P, CH, H, W], F32)
        wv_hi = sb("wv_hi", [P, CH, C], F32R)
        wv_lo = sb("wv_lo", [P, CH, C], F32R)
        wqk_hi = sb("wqk_hi", [P, CH, P], F32R)
        wqk_lo = sb("wqk_lo", [P, CH, P], F32R)
        split_hi = sb("split_hi", [P, 2, 2, CH, P], F32R)
        split_lo = sb("split_lo", [P, 2, 2, CH, P], F32R)
        s_row = sb("s_row", [P, HALF, 64], F32)
        s_col = sb("s_col", [P, HALF, 64], F32)
        pt = sb("pt", [P, 2, 2, SET, P], F16)
        ident = sb("ident", [P, P], F32)
        own = sb("own", [P, 64], F32)
        neg_inf = sb("neg_inf", [P, 1], F32)
        zero = sb("zero", [P, 1], F32)
        tick = sb("tick", [P, 2], F32)
        bqk_sb = sb("bqk_sb", [P, 1], F32)
        gamma_sb = sb("gamma_sb", [P, 1], F32)
        bv_sb = sb("bv_sb", [P, CH], F32)
        gbv = sb("gbv", [P, CH], F32)
        gsc = sb("gsc", [P, 1], F32)
        l1 = sb("l1", [P, CH], F32)
        l1p = sb("l1p", [P, 1], F32)
        l1_all = sb("l1_all", [P, 1], F32)
        amax_u = sb("amax_u", [P, UNITS], F32)
        amax_p = sb("amax_p", [P, 1], F32)
        amax_all = sb("amax_all", [P, 1], F32)
        bound = sb("bound", [P, 1], F32)
        expo = sb("expo", [P, 1], I32)
        v_mul = sb("v_mul", [P, 1], F32)
        v_inv = sb("v_inv", [P, 1], F32)
        out_mul = sb("out_mul", [P, 1], F32)
        m_row = sb("m_row", [P, HALF], F32)
        m_col = sb("m_col", [P, HALF], F32)
        t_row = sb("t_row", [P, HALF], F32)
        mj_row = sb("mj_row", [P, HALF], F32)
        mj_col = sb("mj_col", [P, HALF], F32)
        r_row = sb("r_row", [P, HALF], F32)
        r_col = sb("r_col", [P, HALF], F32)

        def shared(*tensors):
            made = []
            for name, shape, dt in tensors[:-1]:
                with nc.sbuf_tensor(name, shape, dt) as t:
                    made.append(t)
            name, shape, dt = tensors[-1]
            return made + [sb(name, shape, dt)]

        q_parts, v_ring = shared(("q_parts", [P, PIX], F32R), ("v_ring", [P, RING, 2, 2, C], F16))
        q_cols, v_low = shared(("q_cols", [P, HALF, P], F32R), ("v_low", [P, HALF // 2, 2, C], F16))
        with nc.sbuf_tensor("wv_t_sb", [P, CH, C], F32) as wv_t_sb, \
                nc.sbuf_tensor("wv_sb", [P, CH, C], F32) as wv_sb, \
                nc.sbuf_tensor("wqk_sb", [P, CH, P], F32) as wqk_sb:
            pass
        with nc.sbuf_tensor("k_high", [P, PIX], F32R) as k_high, \
                nc.sbuf_tensor("k_low", [P, PIX], F32R) as k_low:
            pass
        v_high = sb("v_high", [P, HALF // 2, 2, C], F16)

        def v_tile(t):
            return v_low[:, t] if t < HALF // 2 else v_high[:, t - HALF // 2]

        ps = ctx.enter_context(nc.psum_tensor("ps", [P, 8, 512], F32))
        S_BANK, OUT_BANK, V_BANK, QK_BANK, PT_BANK = 0, 0, 4, 6, 6

        w_loaded = sem("w_loaded")
        w_split = sem("w_split")
        consts = sem("consts")
        ident_zero = sem("ident_zero")
        ident_made = sem("ident_made")
        own_step = sem("own_step")
        l1_step = sem("l1_step")
        x_loaded = [sem(f"x_loaded{i}") for i in range(UNITS)]
        stored = [sem(f"stored{i}") for i in range(UNITS)]
        hi_split = sem("hi_split")
        lo_split = sem("lo_split")
        qk_mm = sem("qk_mm")
        qk_hi = sem("qk_hi")
        qk_lo = sem("qk_lo")
        k_copied = sem("k_copied")
        q_turned = sem("q_turned")
        s_mm = sem("s_mm")
        s_out = sem("s_out")
        amax_step = sem("amax_step")
        amax_done = sem("amax_done")
        stat = sem("stat")
        scale_step = sem("scale_step")
        shifted = sem("shifted")
        exped = sem("exped")
        probs = sem("probs")
        v_mm = sem("v_mm")
        v_hi = sem("v_hi")
        v_lo = sem("v_lo")
        v_stored = sem("v_stored")
        col_loaded = [sem(f"col_loaded{i}") for i in range(RING)]
        biased = sem("biased")
        pt_mm = sem("pt_mm")
        pt_hi = sem("pt_hi")
        pt_lo = sem("pt_lo")
        out_mm = sem("out_mm")
        added = sem("added")

        def ap(base, dims):
            return bass.AP(base.tensor, base.offset, [base.ap[0], *[list(d) for d in dims]])

        def x_rows(r, n):
            return ap(xs[:, 0, r, :], [(HALF * W, 2 * CH), (1, n * W)])

        def x_tiles(j):
            return ap(xs[:, 0, 2 * j, :], [(W, 2), (HALF * W, 2 * CH), (1, W)])

        def split_slot(part, s):
            return part[:, s % 2].rearrange("p r c (a w) -> p r (c a) w", a=2)

        def unit_pixels(part, i):
            return part[:, ROWS * P * i:ROWS * P * (i + 1)]

        def col_keys(t, part):
            return ap(part[:, t:t + 1], [(HALF, 2), (1, 2), (W, H)])

        def unit_pairs(t, b, i):
            chans = t[b].rearrange("(c p) h w -> p c h w", p=P)
            rows = [slice(a * HALF + ROWS * i, a * HALF + ROWS * (i + 1)) for a in range(2)]
            return [(chans[:, :, r, :].rearrange("p c h w -> p c (h w)"),
                     xs[:, :, r, :].rearrange("p c h w -> p c (h w)")) for r in rows]

        def over_line(stats):
            return stats[:].unsqueeze(2).to_broadcast([P, HALF, 64])

        def transposed(g, a, k):
            pairs = ps[64 * k:64 * k + 64, PT_BANK + g % 2, :].rearrange("p (i n) -> p i n", n=P)
            return pairs[:, :, 64 * a:64 * a + 64]

        def placed(g, part, a, k):
            pairs = pt[64 * a:64 * a + 64, g % 2, part].rearrange("p (i k) n -> p i k n", k=2)
            return pairs[:, :, k, 64 * a:64 * a + 64]

        def slot_free(eng, b, s):
            if s >= SPLITS + 2:
                eng.wait_ge(v_mm, b * HALF + 2 * (s - SPLITS - 2) + 2)
            elif s >= 2:
                eng.wait_ge(qk_mm, b * SPLITS + s - 1)

        block = ctx.enter_context(nc.Block())

        @block.sync
        def _(sp):
            def load(b, i):
                for src, dst in unit_pairs(x, b, i):
                    sp.dma_start(dst, src).then_inc(x_loaded[i], 16)

            sp.dma_start(wqk_sb[:], wqk_t.rearrange("(c p) n -> p c n", p=P)).then_inc(w_loaded, 16)
            sp.dma_start(bqk_sb[:], bqk).then_inc(w_loaded, 16)
            sp.dma_start(gamma_sb[:], gamma).then_inc(w_loaded, 16)
            sp.dma_start(bv_sb[:], bv).then_inc(w_loaded, 16)
            load(0, 0)
            sp.dma_start(wv_t_sb[:], wv_t.rearrange("(c p) n -> p c n", p=P)).then_inc(w_loaded, 16)
            sp.dma_start(wv_sb[:], wv.rearrange("(c p) n -> p c n", p=P)).then_inc(w_loaded, 16)
            for i in range(1, UNITS):
                load(0, i)

            def image(b, following):
                for i in range(UNITS):
                    for part, made in ((k_high, qk_hi), (k_low, qk_lo)):
                        sp.wait_ge(made, b * UNITS + i + 1)
                        sp.dma_start(unit_pixels(part[0:64], i).bitcast(F32),
                                     unit_pixels(part[64:128], i).bitcast(F32)).then_inc(k_copied, 16)
                for t in range(HALF):
                    sp.wait_ge(v_hi, b * HALF + t + 1)
                    sp.wait_ge(v_lo, b * HALF + t + 1)
                    for a in range(2):
                        sp.dma_start(v_dram[2 * t + a, 0:W, :],
                                     v_tile(t)[64 * a:64 * a + 64].rearrange("p s c -> p (s c)")
                                     ).then_inc(v_stored, 16)
                sp.wait_ge(v_stored, b * (HALF * 32) + HALF * 32)
                for n in range(HALF // 2):
                    if n >= RING:
                        sp.wait_ge(out_mm, b * TILES + COL_FROM + 2 * (n - RING) + 2)
                    for a in range(2):
                        sp.dma_start(
                            v_ring[64 * a:64 * a + 64, n % RING].rearrange("p t s c -> p (t s c)"),
                            v_dram[:, a * HALF + 2 * n:a * HALF + 2 * n + 2, :].rearrange("h t c -> h (t c)"),
                        ).then_inc(col_loaded[n % RING], 16)
                for i in range(UNITS + LAG):
                    if i < UNITS:
                        sp.wait_ge(added, b * TILES + max(COL_TO, HALF + ROWS * (i + 1)))
                        for dst, src in unit_pairs(out, b, i):
                            sp.dma_start(dst, src).then_inc(stored[i], 16)
                    if i >= LAG and following:
                        sp.wait_ge(stored[i - LAG], b * 32 + 32)
                        load(b + 1, i - LAG)

            with sp.Fori(0, B - 1) as b:
                image(b, True)
            image(B - 1, False)
            for i in range(UNITS):
                sp.wait_ge(stored[i], 32 * B)

        @block.tensor
        def _(pe):
            pe.wait_ge(w_split, 4)
            pe.wait_ge(consts, 3)
            pe.wait_ge(ident_made, 1)

            def products(dst, chunks):
                for c, (lh, ll, rh, rl) in enumerate(chunks):
                    pe.matmul(dst, lh, rh, start=(c == 0), stop=False)
                    pe.matmul(dst, lh, rl, start=False, stop=False)
                    last = pe.matmul(dst, ll, rh, start=False, stop=(c == CH - 1))
                return last

            def split_ready(b, s):
                pe.wait_ge(hi_split, b * 2 * SPLITS + s + 1)
                pe.wait_ge(lo_split, b * 2 * SPLITS + s + 1)

            with pe.Fori(0, B) as b:
                for s in range(SPLITS):
                    if s % 2 == 0 and s >= 4:
                        pe.wait_ge(qk_lo, b * UNITS + s // 2 - 1)
                    split_ready(b, s)
                    dst = ps[:, QK_BANK + s // 2 % 2, 256 * (s % 2):256 * (s % 2) + 256]
                    products(dst, [(wqk_hi[:, c], wqk_lo[:, c], split_hi[:, s % 2, :, c], split_lo[:, s % 2, :, c])
                                   for c in range(CH)]).then_inc(qk_mm, 1)
                pe.wait_ge(qk_lo, b * UNITS + UNITS)
                pe.wait_ge(k_copied, b * (32 * UNITS) + 32 * UNITS)
                pe.wait_ge(q_turned, b * UNITS + UNITS)
                for n in range(2 * GROUPS):
                    if n >= 2:
                        pe.wait_ge(s_out, b * 2 * GROUPS + n - 1)
                    for k in range(4):
                        t = 4 * (n % GROUPS) + k
                        dst = ps[:, S_BANK + 2 * (n % 2) + k // 2, 256 * (k % 2):256 * (k % 2) + 256]
                        pair = t - k % 2
                        if n < GROUPS:
                            queries = q_parts[:, P * t:P * t + P]
                            keys = [part[:, P * pair:P * pair + 2 * P] for part in (k_high, k_low)]
                        else:
                            queries = q_cols[:, t]
                            keys = [col_keys(pair, part) for part in (k_high, k_low)]
                        pe.matmul(dst, queries, keys[0], start=True, stop=False)
                        last = pe.matmul(dst, queries, keys[1], start=False, stop=True)
                    last.then_inc(s_mm, 1)
                for t in range(HALF):
                    slot = t // 2 % 2
                    if t % 2 == 0:
                        split_ready(b, SPLITS + t // 2)
                    if t >= 2:
                        pe.wait_ge(v_lo, b * HALF + t - 1)
                    last = products(ps[:, V_BANK + t % 2, :],
                                    [(split_hi[:, slot, t % 2, c], split_lo[:, slot, t % 2, c], wv_hi[:, c],
                                      wv_lo[:, c]) for c in range(CH)])
                    last.then_inc(v_mm, 1)

                def transposes(g):
                    kind, n = APPLY[g]
                    src = s_row if kind == "row" else s_col
                    for k in range(SET // 2):
                        t = SET * n + 2 * k
                        last = pe.transpose(ps[:, PT_BANK + g % 2, P * k:P * k + P],
                                            src[:, t:t + 2, :].rearrange("p k u -> p (k u)"), ident[:])
                    last.then_inc(pt_mm, 1)

                pe.wait_ge(probs, b * 2 + 2)
                transposes(0)
                for g, (kind, n) in enumerate(APPLY):
                    if g + 1 < len(APPLY):
                        transposes(g + 1)
                    pe.wait_ge(pt_hi, b * len(APPLY) + g + 1)
                    pe.wait_ge(pt_lo, b * len(APPLY) + g + 1)
                    for k in range(SET):
                        t, i = SET * n + k, SET * g + k
                        if i >= 4:
                            pe.wait_ge(added, b * TILES + i - 3)
                        if kind == "row":
                            v = v_tile(t)
                        else:
                            turn, slot = divmod(t // 2, RING)
                            if t % 2 == 0:
                                pe.wait_ge(col_loaded[slot], b * (HALF // 2 // RING * 32) + (turn + 1) * 32)
                            v = v_ring[:, slot, t % 2]
                        for c in range(CH):
                            if kind == "row":
                                dst = ps[:, OUT_BANK + i % 4, P * c:P * c + P]
                            else:
                                dst = ap(ps[:, OUT_BANK + i % 4, 64 * c:64 * c + 1], [(256, 2), (1, 64)])
                            v_high_part, v_low_part = (v[:, part, P * c:P * c + P] for part in range(2))
                            p_high, p_low = (pt[:, g % 2, part, k] for part in range(2))
                            pe.matmul(dst, v_high_part, p_high, start=True, stop=False)
                            pe.matmul(dst, v_high_part, p_low, start=False, stop=False)
                            last = pe.matmul(dst, v_low_part, p_high, start=False, stop=True)
                        last.then_inc(out_mm, 1)

        @block.scalar
        def _(act):
            act.wait_ge(w_loaded, 16 * 6)
            act.activation(wqk_hi[:], wqk_sb[:], ACT.Copy).then_inc(w_split, 1)
            act.activation(wv_hi[:], wv_t_sb[:], ACT.Copy).then_inc(w_split, 1)
            act.wait_ge(w_split, 4)
            act.wait_ge(l1_step, 1)

            def split(b, s):
                j = s % SPLITS
                if s < SPLITS and j % 2 == 0:
                    act.wait_ge(x_loaded[j // 2], b * 32 + 32)
                slot_free(act, b, s)
                act.activation(split_slot(split_hi, s), x_tiles(j), ACT.Copy).then_inc(hi_split, 1)

            with act.Fori(0, B) as b:
                split(b, 0)
                for i in range(UNITS):
                    split(b, 2 * i + 1)
                    if i < UNITS - 1:
                        split(b, 2 * i + 2)
                    act.wait_ge(qk_mm, b * SPLITS + 2 * i + 2)
                    for lo, part in ((0, q_parts), (64, k_high)):
                        last = act.activation(unit_pixels(part[lo:lo + 64], i), ps[lo:lo + 64, QK_BANK + i % 2, :],
                                              ACT.Identity, bias=bqk_sb[lo:lo + 64, :])
                    last.then_inc(qk_hi, 1)
                split(b, SPLITS)
                split(b, SPLITS + 1)
                for n in range(2 * GROUPS):
                    act.wait_ge(s_mm, b * 2 * GROUPS + n + 1)
                    dst = s_row if n < GROUPS else s_col
                    tile_step, half_step = (P, 64) if n < GROUPS else (64, P)
                    for a in range(2):
                        src = ap(ps[64 * a:64 * a + 64, S_BANK + 2 * (n % 2), half_step * a:half_step * a + 1],
                                 [(512, 2), (256 + tile_step, 2), (1, 64)])
                        t = 4 * (n % GROUPS)
                        last = act.activation(
                            dst[64 * a:64 * a + 64, t:t + 4, :].rearrange("p (i k) u -> p i k u", i=2), src, ACT.Copy)
                    last.then_inc(s_out, 1)
                act.wait_ge(scale_step, b * 4 + 3)
                for j in range(SPLITS):
                    if 1 <= j < SPLITS - 1:
                        split(b, SPLITS + j + 1)
                    for t in (2 * j, 2 * j + 1):
                        act.wait_ge(v_mm, b * HALF + t + 1)
                        act.activation(v_tile(t)[:, 0, :], ps[:, V_BANK + t % 2, :], ACT.Copy,
                                       scale=v_mul[:, 0:1]).then_inc(v_hi, 1)
                    if j in (EXP_AT, EXP_AT + 1):
                        n = j - EXP_AT
                        act.wait_ge(shifted, b * 2 + n + 1)
                        s = (s_row, s_col)[n]
                        act.activation(s[:], s[:], ACT.Exp).then_inc(exped, 1)
                for g in range(len(APPLY)):
                    act.wait_ge(pt_mm, b * len(APPLY) + g + 1)
                    if g >= 2:
                        act.wait_ge(out_mm, b * TILES + SET * (g - 1))
                    for k in range(2):
                        for a in range(2):
                            last = act.activation(placed(g, 0, a, k), transposed(g, a, k), ACT.Copy)
                    last.then_inc(pt_hi, 1)

        @block.vector
        def _(dve):
            dve.memset(pt[:], 0.0).then_inc(consts, 1)
            dve.memset(neg_inf[:], NEG_INF).then_inc(consts, 1)
            dve.wait_ge(w_loaded, 16 * 6)
            dve.wait_ge(w_split, 2)
            dve.tensor_tensor(wqk_lo[:], wqk_sb[:], wqk_hi[:].bitcast(F32), ALU.subtract).then_inc(w_split, 1)
            dve.tensor_tensor(wv_lo[:], wv_t_sb[:], wv_hi[:].bitcast(F32), ALU.subtract).then_inc(w_split, 1)
            dve.tensor_reduce(l1[:], wv_sb[:], AX_X, ALU.add, apply_absolute_value=True).then_inc(l1_step, 1)
            dve.wait_ge(l1_step, 1)
            dve.tensor_reduce(l1p[:], l1[:], AX_X, ALU.max).then_inc(l1_step, 1)
            dve.tensor_scalar(gbv[:], bv_sb[:], gamma_sb[:, 0:1], None, ALU.mult).then_inc(consts, 1)
            dve.tensor_scalar(gsc[:], gamma_sb[:], 1.0 / P_SCALE, None, ALU.mult).then_inc(l1_step, 1)
            dve.wait_ge(l1_step, 4)
            dve.wait_ge(own_step, 4)
            dve.wait_ge(consts, 3)

            def split(b, s):
                j = s % SPLITS
                dve.wait_ge(hi_split, b * 2 * SPLITS + s + 1)
                if s < SPLITS and j % 2 == 0:
                    dve.wait_ge(x_loaded[j // 2], b * 32 + 32)
                slot_free(dve, b, s)
                dve.tensor_tensor(split_slot(split_lo, s), x_tiles(j), split_slot(split_hi, s).bitcast(F32),
                                  ALU.subtract).then_inc(lo_split, 1)

            def swap(dst, src):
                for q, r in ((0, 0), (1, 2), (2, 1), (3, 3)):
                    last = dve.transpose(dst[32 * r:32 * r + 32, :], src[32 * q:32 * q + 32, :])
                return last

            with dve.Fori(0, B) as b:
                def step(n):
                    dve.wait_ge(stat, b * STATS + n)

                split(b, 0)
                for i in range(UNITS):
                    split(b, 2 * i + 1)
                    if i < UNITS - 1:
                        split(b, 2 * i + 2)
                    dve.wait_ge(qk_hi, b * UNITS + i + 1)
                    for lo, dst, high in ((0, q_parts[64:128], q_parts[0:64]), (64, k_low[64:128], k_high[64:128])):
                        last = dve.scalar_tensor_tensor(
                            out=unit_pixels(dst, i), in0=ps[lo:lo + 64, QK_BANK + i % 2, :],
                            scalar=bqk_sb[lo:lo + 64, :], in1=unit_pixels(high, i).bitcast(F32),
                            op0=ALU.add, op1=ALU.subtract)
                    last.then_inc(qk_lo, 1)
                split(b, SPLITS)
                split(b, SPLITS + 1)
                for i in range(UNITS):
                    dve.tensor_reduce(amax_u[:, i:i + 1], x_rows(ROWS * i, ROWS), mybir.AxisListType.XY, ALU.max,
                                      apply_absolute_value=True).then_inc(amax_step, 1)
                dve.wait_ge(amax_step, b * (UNITS + 1) + UNITS)
                dve.tensor_reduce(amax_p[:], amax_u[:], AX_X, ALU.max).then_inc(amax_step, 1)
                dve.wait_ge(amax_done, b + 1)
                dve.tensor_scalar(bound[:], amax_all[:], l1_all[:, 0:1], 2.0 ** -90, ALU.mult,
                                  ALU.max).then_inc(scale_step, 1)
                dve.wait_ge(scale_step, b * 4 + 1)
                dve.tensor_scalar(expo[:], bound[:].bitcast(I32), 0x7F800000, None,
                                  ALU.bitwise_and).then_inc(scale_step, 1)
                dve.wait_ge(scale_step, b * 4 + 2)
                dve.tensor_scalar(v_inv[:].bitcast(I32), expo[:], float(-V_EXP * MANT), None, ALU.add)
                dve.tensor_scalar(v_mul[:].bitcast(I32), expo[:], -1.0, float((254 + V_EXP) * MANT), ALU.mult,
                                  ALU.add).then_inc(scale_step, 1)
                dve.wait_ge(scale_step, b * 4 + 3)
                dve.tensor_scalar(out_mul[:], v_inv[:], gsc[:, 0:1], None, ALU.mult).then_inc(scale_step, 1)

                for j in range(SPLITS):
                    if 1 <= j < SPLITS - 1:
                        split(b, SPLITS + j + 1)
                    for t in (2 * j, 2 * j + 1):
                        dve.wait_ge(v_hi, b * HALF + t + 1)
                        dve.scalar_tensor_tensor(out=v_tile(t)[:, 1, :], in0=ps[:, V_BANK + t % 2, :],
                                                 scalar=v_mul[:, 0:1], in1=v_tile(t)[:, 0, :], op0=ALU.mult,
                                                 op1=ALU.subtract).then_inc(v_lo, 1)
                    if j == 0:
                        dve.wait_ge(s_out, b * 2 * GROUPS + 2 * GROUPS)
                        dve.tensor_reduce(m_row[:], s_row[:], AX_X, ALU.max).then_inc(stat, 1)
                        dve.copy_predicated(s_col[:], ap(own[:], [(0, HALF), (1, 64)]).bitcast(I32),
                                            ap(neg_inf[:], [(0, HALF), (0, 64)])).then_inc(stat, 1)
                        step(2)
                        dve.tensor_reduce(m_col[:], s_col[:], AX_X, ALU.max).then_inc(stat, 1)
                        step(3)
                        swap(t_row, m_col).then_inc(stat, 1)
                        step(4)
                        dve.tensor_tensor(mj_row[:], m_row[:], t_row[:], ALU.max).then_inc(stat, 1)
                        step(5)
                        swap(mj_col, mj_row).then_inc(stat, 1)
                        step(6)
                    if j in (1, 2):
                        s, m = ((s_row, mj_row), (s_col, mj_col))[j - 1]
                        dve.tensor_tensor(s[:], s[:], over_line(m), ALU.subtract).then_inc(shifted, 1)
                    if j == EXP_AT + 2:
                        dve.wait_ge(exped, b * 2 + 2)
                        dve.tensor_reduce(m_row[:], s_row[:], AX_X, ALU.add)
                        dve.tensor_reduce(m_col[:], s_col[:], AX_X, ALU.add).then_inc(stat, 1)
                        step(7)
                        swap(t_row, m_col).then_inc(stat, 1)
                        step(8)
                        dve.tensor_tensor(mj_row[:], m_row[:], t_row[:], ALU.add).then_inc(stat, 1)
                        step(9)
                        dve.reciprocal(r_row[:], mj_row[:]).then_inc(stat, 1)
                        step(10)
                        dve.tensor_scalar(mj_row[:], r_row[:], P_SCALE, None, ALU.mult).then_inc(stat, 1)
                        step(11)
                        swap(mj_col, mj_row).then_inc(stat, 1)
                        step(12)
                    if j in (EXP_AT + 3, EXP_AT + 4):
                        s, r = ((s_row, mj_row), (s_col, mj_col))[j - EXP_AT - 3]
                        dve.tensor_tensor(s[:], s[:], over_line(r), ALU.mult).then_inc(probs, 1)

                def low(g):
                    dve.wait_ge(pt_hi, b * len(APPLY) + g + 1)
                    if g >= 2:
                        dve.wait_ge(out_mm, b * TILES + SET * (g - 1))
                    for k in range(2):
                        for a in range(2):
                            last = dve.tensor_tensor(placed(g, 1, a, k), transposed(g, a, k), placed(g, 0, a, k),
                                                     ALU.subtract)
                    last.then_inc(pt_lo, 1)

                dve.wait_ge(biased, b * SPLITS + SPLITS)
                dve.wait_ge(scale_step, b * 4 + 4)
                low(0)
                for g, (kind, n) in enumerate(APPLY):
                    if g + 1 < len(APPLY):
                        low(g + 1)
                    for k in range(SET):
                        t, i = SET * n + k, SET * g + k
                        if i in (COL_FROM, COL_TO):
                            dve.wait_ge(added, b * TILES + i)
                        dve.wait_ge(out_mm, b * TILES + i + 1)
                        bank = ps[:, OUT_BANK + i % 4, :]
                        if kind == "row":
                            sums, place = bank.rearrange("p (c n) -> p c n", n=64), x_rows(t, 1)
                        else:
                            sums = bank.rearrange("p (a n) -> p a n", a=2)
                            place = ap(xs[:, 0, 0, t:t + 1], [(HALF, 2), (W, CH * H)])
                        dve.scalar_tensor_tensor(out=place, in0=sums, scalar=out_mul[:, 0:1], in1=place,
                                                 op0=ALU.mult, op1=ALU.add).then_inc(added, 1)

        @block.gpsimd
        def _(pool):
            pool.memset(ident[:], 0.0).then_inc(ident_zero, 1)
            pool.memset(zero[:], 0.0).then_inc(ident_zero, 1)
            pool.memset(own[:], 0.0).then_inc(ident_zero, 1)
            pool.wait_ge(ident_zero, 3)
            pool.affine_select(out=ident[:], in_=ident[:], compare_op=ALU.not_equal, fill=1.0, base=0,
                               pattern=[[-1, P]], channel_multiplier=1).then_inc(ident_made, 1)
            pool.wait_ge(ident_made, 1)
            for q in range(4):
                if q:
                    pool.wait_ge(own_step, q)
                part = own[32 * q:32 * q + 32, :]
                pool.affine_select(out=part, in_=part, compare_op=ALU.not_equal, fill=1.0, base=q % 2,
                                   pattern=[[-1, 64]], channel_multiplier=2).then_inc(own_step, 1)
            pool.wait_ge(own_step, 4)
            pool.wait_ge(l1_step, 2)
            pool.partition_all_reduce(l1_all[:], l1p[:], P, RMAX).then_inc(l1_step, 1)
            pool.wait_ge(consts, 3)
            def wait(semaphore, value, n):
                pool.wait_ge(semaphore, value)
                pool.tensor_tensor(tick[:, n:n + 1], zero[:], zero[:], ALU.add)

            with pool.Fori(0, B) as b:
                for i in range(UNITS):
                    pool.wait_ge(qk_lo, b * UNITS + i + 1)
                    for a in range(2):
                        src = ap(q_parts[:, ROWS * P * i + W * a:ROWS * P * i + W * a + 1],
                                 [(P, ROWS), (HALF, 2), (1, HALF)]).bitcast(F32)
                        dst = ap(q_cols[:, 0, HALF * a + ROWS * i:HALF * a + ROWS * i + 1],
                                 [(1, ROWS), (64, 2), (P, HALF)])
                        last = pool.tensor_tensor(dst, src, ap(zero[:], [(0, ROWS), (0, 2), (0, HALF)]), ALU.add)
                    last.then_inc(q_turned, 1)
                wait(amax_step, b * (UNITS + 1) + UNITS + 1, 0)
                pool.partition_all_reduce(amax_all[:], amax_p[:], P, RMAX).then_inc(amax_done, 1)
                for j in range(SPLITS):
                    pool.wait_ge(hi_split, b * 2 * SPLITS + SPLITS + j + 1)
                    pool.wait_ge(lo_split, b * 2 * SPLITS + SPLITS + j + 1)
                    place = ap(xs[:, 0, 2 * j, :], [(PIX, CH), (HALF * W, 2), (1, 2 * W)])
                    pool.tensor_tensor(place, place, ap(gbv[:], [(1, CH), (0, 2), (0, 2 * W)]),
                                       ALU.add).then_inc(biased, 1)


_OUT = ((16, 512, 64, 64), "float32")


def kernel(x, L0_conv_Wq, L0_conv_bq, L0_conv_Wk, L0_conv_bk, L0_conv_Wv, L0_conv_bv, L0_conv_gamma):
    import numpy as np
    import concourse.bacc as bacc
    from concourse.bass_utils import run_bass_kernel_spmd

    nc = bacc.Bacc("TRN2", target_bir_lowering=False, num_devices=1)
    wq, wk, wv = (np.asarray(w) for w in (L0_conv_Wq, L0_conv_Wk, L0_conv_Wv))
    given = {
        "x": np.asarray(x),
        "wqk_t": np.concatenate([wq.T, wk.T], axis=1),
        "bqk": np.concatenate([np.asarray(L0_conv_bq), np.asarray(L0_conv_bk)]).reshape(-1, 1),
        "wv_t": wv.T,
        "wv": wv,
        "bv": np.asarray(L0_conv_bv).reshape(-1, 128).T,
        "gamma": np.broadcast_to(np.asarray(L0_conv_gamma).reshape(1, 1), (128, 1)),
    }
    arrays = {f"{name}_dram": np.ascontiguousarray(a) for name, a in given.items()}
    args = [nc.dram_tensor(name, a.shape, mybir.dt.from_np(a.dtype), kind="ExternalInput").ap()
            for name, a in arrays.items()]
    shape, dtype = _OUT
    args.append(nc.dram_tensor("out_dram", shape, mybir.dt.from_np(np.dtype(dtype)), kind="ExternalOutput").ap())
    criss_cross(nc, *args)
    return run_bass_kernel_spmd(nc, [arrays], core_ids=[0]).results[0]["out_dram"]
```

```python
from contextlib import ExitStack

import concourse.bass as bass
from concourse import mybir

ALU = mybir.AluOpType
ACT = mybir.ActivationFunctionType
F32 = mybir.dt.float32
F32R = mybir.dt.float32r
F16 = mybir.dt.float16
I32 = mybir.dt.int32
AX_X = mybir.AxisListType.X
RMAX = bass.bass_isa.ReduceOp.max

P = 128
NEG_INF = -1e30
P_SCALE = 2.0 ** 12
V_EXP = 14
MANT = 1 << 23


def criss_cross(nc, x, wqk_t, bqk, wv_t, wv, bv, gamma, out):
    B, C, H, W = x.shape
    CH = C // P
    CQ = wqk_t.shape[1] // 2
    HALF = H // 2
    PIX = H * W
    assert CQ == 64 and H == W == 64 and C == CH * P and bqk.shape[0] == P
    UNITS = 8
    ROWS = HALF // UNITS
    SPLITS = HALF // 2
    GROUPS = HALF // 4
    SET = 8
    SETS = HALF // SET
    APPLY = [("row", 0)] + [("col", g) for g in range(SETS)] + [("row", g) for g in range(1, SETS)]
    TILES = SET * len(APPLY)
    COL_FROM, COL_TO = 8, 8 + HALF
    LAG = 2
    EXP_AT = 3
    EARLY = 4
    QK_SLOTS = 4
    POOL_QK = (0, 4, 8, 12)
    AHEAD = 3
    STATS = 12
    RING = 4
    PITCH = W + 2

    v_dram = nc.dram_tensor("v_dram", (H, PITCH, 2 * C), F16, kind="Internal").ap()

    with ExitStack() as ctx:
        def sb(name, shape, dt):
            return ctx.enter_context(nc.sbuf_tensor(name, shape, dt))

        def sem(name):
            return ctx.enter_context(nc.semaphore(name))

        xs = sb("xs", [P, CH, H, W], F32)
        wv_hi = sb("wv_hi", [P, CH, C], F32R)
        wv_lo = sb("wv_lo", [P, CH, C], F32R)
        wqk_hi = sb("wqk_hi", [P, CH, P], F32R)
        wqk_lo = sb("wqk_lo", [P, CH, P], F32R)
        split_lo = sb("split_lo", [P, 2, 2, CH, P], F32R)
        s_row = sb("s_row", [P, HALF, 64], F32)
        s_col = sb("s_col", [P, HALF, 64], F32)
        pt = sb("pt", [P, 2, 2, SET, P], F16)
        ident = sb("ident", [P, P], F32)
        own = sb("own", [P, 64], F32)
        neg_inf = sb("neg_inf", [P, 1], F32)
        zero = sb("zero", [P, 1], F32)
        tick = sb("tick", [P, 2], F32)
        bqk_sb = sb("bqk_sb", [P, 1], F32)
        gamma_sb = sb("gamma_sb", [P, 1], F32)
        bv_sb = sb("bv_sb", [P, CH], F32)
        gbv = sb("gbv", [P, CH], F32)
        gsc = sb("gsc", [P, 1], F32)
        l1 = sb("l1", [P, CH], F32)
        l1p = sb("l1p", [P, 1], F32)
        l1_all = sb("l1_all", [P, 1], F32)
        amax_u = sb("amax_u", [P, UNITS], F32)
        amax_p = sb("amax_p", [P, 1], F32)
        amax_all = sb("amax_all", [P, 1], F32)
        bound = sb("bound", [P, 1], F32)
        expo = sb("expo", [P, 1], I32)
        v_mul = sb("v_mul", [P, 1], F32)
        v_inv = sb("v_inv", [P, 1], F32)
        out_mul = sb("out_mul", [P, 1], F32)
        m_row = sb("m_row", [P, HALF], F32)
        m_col = sb("m_col", [P, HALF], F32)
        t_row = sb("t_row", [P, HALF], F32)
        mj_row = sb("mj_row", [P, HALF], F32)
        mj_col = sb("mj_col", [P, HALF], F32)
        r_row = sb("r_row", [P, HALF], F32)
        r_col = sb("r_col", [P, HALF], F32)

        def shared(*tensors):
            made = []
            for name, shape, dt in tensors[:-1]:
                with nc.sbuf_tensor(name, shape, dt) as t:
                    made.append(t)
            name, shape, dt = tensors[-1]
            return made + [sb(name, shape, dt)]

        pt_whole, split_hi = shared(("pt_whole", [P, 2, SET, 64], F32), ("split_hi", [P, 2, 2, CH, P], F32R))
        q_parts, v_ring = shared(("q_parts", [P, PIX], F32R), ("v_ring", [P, RING, 2, 2, C], F16))
        with nc.sbuf_tensor("q_cols", [P, HALF, P], F32R) as q_cols, \
                nc.sbuf_tensor("more_hi", [P, 2, 2, CH, P], F32R) as more_hi, \
                nc.sbuf_tensor("more_lo", [P, 2, 2, CH, P], F32R) as more_lo:
            pass
        v_low = sb("v_low", [P, HALF // 2, 2, C], F16)
        with nc.sbuf_tensor("wv_t_sb", [P, CH, C], F32) as wv_t_sb, \
                nc.sbuf_tensor("wv_sb", [P, CH, C], F32) as wv_sb, \
                nc.sbuf_tensor("wqk_sb", [P, CH, P], F32) as wqk_sb:
            pass
        with nc.sbuf_tensor("k_high", [P, PIX], F32R) as k_high, \
                nc.sbuf_tensor("k_low", [P, PIX], F32R) as k_low:
            pass
        v_high = sb("v_high", [P, HALF // 2, 2, C], F16)

        def v_tile(t):
            return v_low[:, t] if t < HALF // 2 else v_high[:, t - HALF // 2]

        ps = ctx.enter_context(nc.psum_tensor("ps", [P, 8, 512], F32))
        S_BANK, OUT_BANK, V_BANK, QK_BANK, PT_BANK = 0, 0, 4, 6, 4
        V_BANKS = 4

        w_loaded = sem("w_loaded")
        w_split = sem("w_split")
        consts = sem("consts")
        ident_zero = sem("ident_zero")
        ident_made = sem("ident_made")
        own_step = sem("own_step")
        l1_step = sem("l1_step")
        x_loaded = [sem(f"x_loaded{i}") for i in range(UNITS)]
        stored = [sem(f"stored{i}") for i in range(UNITS)]
        hi_split = sem("hi_split")
        lo_split = sem("lo_split")
        lo_split_pool = sem("lo_split_pool")
        qk_mm = sem("qk_mm")
        qk_hi = sem("qk_hi")
        qk_lo = sem("qk_lo")
        k_copied = sem("k_copied")
        q_turned = sem("q_turned")
        s_mm = sem("s_mm")
        s_out = sem("s_out")
        amax_step = sem("amax_step")
        amax_done = sem("amax_done")
        stat = sem("stat")
        scale_step = sem("scale_step")
        shifted = sem("shifted")
        exped = sem("exped")
        probs = sem("probs")
        v_mm = sem("v_mm")
        v_hi = sem("v_hi")
        v_lo = sem("v_lo")
        v_stored = sem("v_stored")
        col_loaded = [sem(f"col_loaded{i}") for i in range(RING)]
        biased = sem("biased")
        pt_mm = sem("pt_mm")
        pt_out = sem("pt_out")
        pt_hi = sem("pt_hi")
        pt_lo = sem("pt_lo")
        out_mm = sem("out_mm")
        added = sem("added")

        def ap(base, dims):
            return bass.AP(base.tensor, base.offset, [base.ap[0], *[list(d) for d in dims]])

        def x_rows(r, n):
            return ap(xs[:, 0, r, :], [(HALF * W, 2 * CH), (1, n * W)])

        def x_tiles(j):
            return ap(xs[:, 0, 2 * j, :], [(W, 2), (HALF * W, 2 * CH), (1, W)])

        def slot(part, s):
            if s < SPLITS and s % QK_SLOTS >= 2:
                return {"hi": more_hi, "lo": more_lo}[part][:, s % 2]
            return {"hi": split_hi, "lo": split_lo}[part][:, s % 2]

        def by_row(split):
            return split.rearrange("p r c (a w) -> p r (c a) w", a=2)

        def unit_pixels(part, i):
            return part[:, ROWS * P * i:ROWS * P * (i + 1)]

        def col_keys(t, part):
            return ap(part[:, t:t + 1], [(HALF, 2), (1, 2), (W, H)])

        def unit_pairs(t, b, i):
            chans = t[b].rearrange("(c p) h w -> p c h w", p=P)
            rows = [slice(a * HALF + ROWS * i, a * HALF + ROWS * (i + 1)) for a in range(2)]
            return [(chans[:, :, r, :].rearrange("p c h w -> p c (h w)"),
                     xs[:, :, r, :].rearrange("p c h w -> p c (h w)")) for r in rows]

        def over_line(stats):
            return stats[:].unsqueeze(2).to_broadcast([P, HALF, 64])

        def transposed(g, a, k):
            pairs = ps[64 * k:64 * k + 64, PT_BANK + g % 2, :].rearrange("p (i n) -> p i n", n=P)
            return pairs[:, :, 64 * a:64 * a + 64]

        def placed(g, part, a, k):
            pairs = pt[64 * a:64 * a + 64, g % 2, part].rearrange("p (i k) n -> p i k n", k=2)
            return pairs[:, :, k, 64 * a:64 * a + 64]

        def whole(g, a, k):
            pairs = pt_whole[64 * a:64 * a + 64, g % 2].rearrange("p (i k) n -> p i k n", k=2)
            return pairs[:, :, k]

        def by_pool(s):
            return s >= SPLITS or s in POOL_QK

        DVE_SPLITS = sum(not by_pool(s) for s in range(2 * SPLITS))

        def wait_lo_split(eng, b, s):
            if by_pool(s):
                n = sum(by_pool(r) for r in range(s + 1))
                eng.wait_ge(lo_split_pool, b * (2 * SPLITS - DVE_SPLITS) + n)
            else:
                n = sum(not by_pool(r) for r in range(s + 1))
                eng.wait_ge(lo_split, b * DVE_SPLITS + n)

        def sums_and_place(kind, t, sums):
            if kind == "row":
                return sums.rearrange("p (c n) -> p c n", n=W), x_rows(t, 1)
            return sums.rearrange("p (a n) -> p a n", a=2), ap(xs[:, 0, 0, t:t + 1], [(HALF, 2), (W, CH * H)])

        def split_low(eng, b, s):
            eng.wait_ge(hi_split, b * 2 * SPLITS + s + 1)
            if s < SPLITS:
                eng.wait_ge(x_loaded[s // 2], b * 32 + 32)
            slot_free(eng, b, s)
            eng.tensor_tensor(by_row(slot("lo", s)), x_tiles(s % SPLITS), by_row(slot("hi", s)).bitcast(F32),
                              ALU.subtract).then_inc(lo_split_pool if by_pool(s) else lo_split, 1)

        def slot_free(eng, b, s):
            if s >= SPLITS + 2:
                eng.wait_ge(v_mm, b * HALF + 2 * (s - SPLITS - 2) + 2)
            elif s >= QK_SLOTS:
                eng.wait_ge(qk_mm, b * SPLITS + s - QK_SLOTS + 1)

        block = ctx.enter_context(nc.Block())

        @block.sync
        def _(sp):
            def load(b, i):
                for src, dst in unit_pairs(x, b, i):
                    sp.dma_start(dst, src).then_inc(x_loaded[i], 16)

            sp.dma_start(wqk_sb[:], wqk_t.rearrange("(c p) n -> p c n", p=P)).then_inc(w_loaded, 16)
            sp.dma_start(bqk_sb[:], bqk).then_inc(w_loaded, 16)
            sp.dma_start(gamma_sb[:], gamma).then_inc(w_loaded, 16)
            sp.dma_start(bv_sb[:], bv).then_inc(w_loaded, 16)
            load(0, 0)
            sp.dma_start(wv_t_sb[:], wv_t.rearrange("(c p) n -> p c n", p=P)).then_inc(w_loaded, 16)
            sp.dma_start(wv_sb[:], wv.rearrange("(c p) n -> p c n", p=P)).then_inc(w_loaded, 16)
            for i in range(1, UNITS):
                load(0, i)

            def image(b, following):
                for i in range(UNITS):
                    for part, made in ((k_high, qk_hi), (k_low, qk_lo)):
                        sp.wait_ge(made, b * UNITS + i + 1)
                        sp.dma_start(unit_pixels(part[0:64], i).bitcast(F32),
                                     unit_pixels(part[64:128], i).bitcast(F32)).then_inc(k_copied, 16)
                for t in range(HALF):
                    sp.wait_ge(v_hi, b * HALF + t + 1)
                    sp.wait_ge(v_lo, b * HALF + t + 1)
                    for a in range(2):
                        sp.dma_start(v_dram[2 * t + a, 0:W, :],
                                     v_tile(t)[64 * a:64 * a + 64].rearrange("p s c -> p (s c)")
                                     ).then_inc(v_stored, 16)
                sp.wait_ge(v_stored, b * (HALF * 32) + HALF * 32)
                for n in range(HALF // 2):
                    if n >= RING:
                        sp.wait_ge(out_mm, b * TILES + COL_FROM + 2 * (n - RING) + 2)
                    for a in range(2):
                        sp.dma_start(
                            v_ring[64 * a:64 * a + 64, n % RING].rearrange("p t s c -> p (t s c)"),
                            v_dram[:, a * HALF + 2 * n:a * HALF + 2 * n + 2, :].rearrange("h t c -> h (t c)"),
                        ).then_inc(col_loaded[n % RING], 16)
                for i in range(UNITS + LAG):
                    if i < UNITS:
                        sp.wait_ge(added, b * TILES + max(COL_TO, HALF + ROWS * (i + 1)))
                        for dst, src in unit_pairs(out, b, i):
                            sp.dma_start(dst, src).then_inc(stored[i], 16)
                    if i >= LAG and following:
                        sp.wait_ge(stored[i - LAG], b * 32 + 32)
                        load(b + 1, i - LAG)

            with sp.Fori(0, B - 1) as b:
                image(b, True)
            image(B - 1, False)
            for i in range(UNITS):
                sp.wait_ge(stored[i], 32 * B)

        @block.tensor
        def _(pe):
            pe.wait_ge(w_split, 4)
            pe.wait_ge(consts, 3)
            pe.wait_ge(ident_made, 1)

            def products(dst, chunks):
                for c, (lh, ll, rh, rl) in enumerate(chunks):
                    pe.matmul(dst, lh, rh, start=(c == 0), stop=False)
                    pe.matmul(dst, lh, rl, start=False, stop=False)
                    last = pe.matmul(dst, ll, rh, start=False, stop=(c == CH - 1))
                return last

            def split_ready(b, s):
                pe.wait_ge(hi_split, b * 2 * SPLITS + s + 1)
                wait_lo_split(pe, b, s)

            def v_tiles(b, start, end):
                for t in range(start, end):
                    hi, lo = (slot(part, SPLITS + t // 2)[:, t % 2] for part in ("hi", "lo"))
                    if t % 2 == 0:
                        split_ready(b, SPLITS + t // 2)
                    if t >= V_BANKS:
                        pe.wait_ge(v_lo, b * HALF + t - V_BANKS + 1)
                    elif t >= V_BANKS - 2:
                        pe.wait_ge(qk_lo, b * UNITS + UNITS - (V_BANKS - 1 - t))
                    last = products(ps[:, V_BANK + t % V_BANKS, :],
                                    [(hi[:, c], lo[:, c], wv_hi[:, c], wv_lo[:, c]) for c in range(CH)])
                    last.then_inc(v_mm, 1)

            with pe.Fori(0, B) as b:
                for s in range(SPLITS):
                    if s % 2 == 0 and s >= 4:
                        pe.wait_ge(qk_lo, b * UNITS + s // 2 - 1)
                    split_ready(b, s)
                    dst = ps[:, QK_BANK + s // 2 % 2, 256 * (s % 2):256 * (s % 2) + 256]
                    hi, lo = slot("hi", s), slot("lo", s)
                    products(dst, [(wqk_hi[:, c], wqk_lo[:, c], hi[:, :, c], lo[:, :, c]) for c in range(CH)]).then_inc(qk_mm, 1)
                v_tiles(b, 0, EARLY)
                pe.wait_ge(qk_lo, b * UNITS + UNITS)
                pe.wait_ge(k_copied, b * (32 * UNITS) + 32 * UNITS)
                pe.wait_ge(q_turned, b * UNITS + UNITS)
                for n in range(2 * GROUPS):
                    if n >= 2:
                        pe.wait_ge(s_out, b * 2 * GROUPS + n - 1)
                    for k in range(4):
                        t = 4 * (n % GROUPS) + k
                        dst = ps[:, S_BANK + 2 * (n % 2) + k // 2, 256 * (k % 2):256 * (k % 2) + 256]
                        pair = t - k % 2
                        if n < GROUPS:
                            queries = q_parts[:, P * t:P * t + P]
                            keys = [part[:, P * pair:P * pair + 2 * P] for part in (k_high, k_low)]
                        else:
                            queries = q_cols[:, t]
                            keys = [col_keys(pair, part) for part in (k_high, k_low)]
                        pe.matmul(dst, queries, keys[0], start=True, stop=False)
                        last = pe.matmul(dst, queries, keys[1], start=False, stop=True)
                    last.then_inc(s_mm, 1)
                v_tiles(b, EARLY, HALF)
                def transposes(g):
                    kind, n = APPLY[g]
                    src = s_row if kind == "row" else s_col
                    if g < 2:
                        pe.wait_ge(v_lo, b * HALF + HALF - V_BANKS + g + 1)
                    for k in range(SET // 2):
                        t = SET * n + 2 * k
                        last = pe.transpose(ps[:, PT_BANK + g % 2, P * k:P * k + P],
                                            src[:, t:t + 2, :].rearrange("p k u -> p (k u)"), ident[:])
                    last.then_inc(pt_mm, 1)

                pe.wait_ge(probs, b * 2 + 2)
                transposes(0)
                for g, (kind, n) in enumerate(APPLY):
                    if g + 1 < len(APPLY):
                        transposes(g + 1)
                    pe.wait_ge(pt_hi, b * len(APPLY) + g + 1)
                    pe.wait_ge(pt_lo, b * len(APPLY) + g + 1)
                    for k in range(SET):
                        t, i = SET * n + k, SET * g + k
                        if i >= 4:
                            pe.wait_ge(added, b * TILES + i - 3)
                        if kind == "row":
                            v = v_tile(t)
                        else:
                            turn, place = divmod(t // 2, RING)
                            if t % 2 == 0:
                                pe.wait_ge(col_loaded[place], b * (HALF // 2 // RING * 32) + (turn + 1) * 32)
                            v = v_ring[:, place, t % 2]
                        for c in range(CH):
                            if kind == "row":
                                dst = ps[:, OUT_BANK + i % 4, P * c:P * c + P]
                            else:
                                dst = ap(ps[:, OUT_BANK + i % 4, 64 * c:64 * c + 1], [(256, 2), (1, 64)])
                            v_high_part, v_low_part = (v[:, part, P * c:P * c + P] for part in range(2))
                            p_high, p_low = (pt[:, g % 2, part, k] for part in range(2))
                            pe.matmul(dst, v_high_part, p_high, start=True, stop=False)
                            pe.matmul(dst, v_high_part, p_low, start=False, stop=False)
                            last = pe.matmul(dst, v_low_part, p_high, start=False, stop=True)
                        last.then_inc(out_mm, 1)

        @block.scalar
        def _(act):
            act.wait_ge(w_loaded, 16 * 6)
            act.activation(wqk_hi[:], wqk_sb[:], ACT.Copy).then_inc(w_split, 1)
            act.activation(wv_hi[:], wv_t_sb[:], ACT.Copy).then_inc(w_split, 1)
            act.wait_ge(w_split, 4)
            act.wait_ge(l1_step, 1)
            act.wait_ge(consts, 3)

            def split(b, s):
                j = s % SPLITS
                if s < SPLITS and j % 2 == 0:
                    act.wait_ge(x_loaded[j // 2], b * 32 + 32)
                slot_free(act, b, s)
                act.activation(by_row(slot("hi", s)), x_tiles(j), ACT.Copy).then_inc(hi_split, 1)

            with act.Fori(0, B) as b:
                for s in range(AHEAD):
                    split(b, s)
                for i in range(UNITS):
                    for s in (2 * i + AHEAD, 2 * i + AHEAD + 1):
                        if s < SPLITS + 2:
                            split(b, s)
                    act.wait_ge(qk_mm, b * SPLITS + 2 * i + 2)
                    for lo, part in ((0, q_parts), (64, k_high)):
                        last = act.activation(unit_pixels(part[lo:lo + 64], i), ps[lo:lo + 64, QK_BANK + i % 2, :],
                                              ACT.Identity, bias=bqk_sb[lo:lo + 64, :])
                    last.then_inc(qk_hi, 1)
                for j in range(2, EARLY):
                    split(b, SPLITS + j)
                for n in range(2 * GROUPS):
                    act.wait_ge(s_mm, b * 2 * GROUPS + n + 1)
                    dst = s_row if n < GROUPS else s_col
                    tile_step, half_step = (P, 64) if n < GROUPS else (64, P)
                    for a in range(2):
                        src = ap(ps[64 * a:64 * a + 64, S_BANK + 2 * (n % 2), half_step * a:half_step * a + 1],
                                 [(512, 2), (256 + tile_step, 2), (1, 64)])
                        t = 4 * (n % GROUPS)
                        last = act.activation(
                            dst[64 * a:64 * a + 64, t:t + 4, :].rearrange("p (i k) u -> p i k u", i=2), src, ACT.Copy)
                    last.then_inc(s_out, 1)
                act.wait_ge(scale_step, b * 4 + 3)
                for j in range(SPLITS):
                    for t in (2 * j, 2 * j + 1):
                        act.wait_ge(v_mm, b * HALF + t + 1)
                        act.activation(v_tile(t)[:, 0, :], ps[:, V_BANK + t % V_BANKS, :], ACT.Copy,
                                       scale=v_mul[:, 0:1]).then_inc(v_hi, 1)
                    if EARLY <= j + 2 < SPLITS:
                        split(b, SPLITS + j + 2)
                    if j % 2 == 1:
                        wait_lo_split(act, b, SPLITS + j)
                        for c in range(CH):
                            place = ap(xs[:, c, ROWS * (j // 2), :], [(HALF * W, 2), (1, ROWS * W)])
                            last = act.activation(place, place, ACT.Identity, bias=gbv[:, c:c + 1])
                        last.then_inc(biased, 1)
                    if j in (EXP_AT, EXP_AT + 1):
                        n = j - EXP_AT
                        act.wait_ge(shifted, b * 2 + n + 1)
                        s = (s_row, s_col)[n]
                        act.activation(s[:], s[:], ACT.Exp).then_inc(exped, 1)

                for g in range(len(APPLY)):
                    act.wait_ge(pt_mm, b * len(APPLY) + g + 1)
                    if g >= 2:
                        act.wait_ge(out_mm, b * TILES + SET * (g - 1))
                        act.wait_ge(pt_lo, b * len(APPLY) + g - 1)
                    for semaphore, dst in ((pt_hi, lambda a, k: placed(g, 0, a, k)),
                                           (pt_out, lambda a, k: whole(g, a, k))):
                        for k in range(2):
                            for a in range(2):
                                last = act.activation(dst(a, k), transposed(g, a, k), ACT.Copy)
                        last.then_inc(semaphore, 1)
                act.wait_ge(pt_lo, b * len(APPLY) + len(APPLY))

        @block.vector
        def _(dve):
            dve.memset(pt[:], 0.0).then_inc(consts, 1)
            dve.memset(neg_inf[:], NEG_INF).then_inc(consts, 1)
            dve.wait_ge(w_loaded, 16 * 6)
            dve.wait_ge(w_split, 2)
            dve.tensor_tensor(wqk_lo[:], wqk_sb[:], wqk_hi[:].bitcast(F32), ALU.subtract).then_inc(w_split, 1)
            dve.tensor_tensor(wv_lo[:], wv_t_sb[:], wv_hi[:].bitcast(F32), ALU.subtract).then_inc(w_split, 1)
            dve.tensor_reduce(l1[:], wv_sb[:], AX_X, ALU.add, apply_absolute_value=True).then_inc(l1_step, 1)
            dve.wait_ge(l1_step, 1)
            dve.tensor_reduce(l1p[:], l1[:], AX_X, ALU.max).then_inc(l1_step, 1)
            dve.tensor_scalar(gbv[:], bv_sb[:], gamma_sb[:, 0:1], None, ALU.mult).then_inc(consts, 1)
            dve.tensor_scalar(gsc[:], gamma_sb[:], 1.0 / P_SCALE, None, ALU.mult).then_inc(l1_step, 1)
            dve.wait_ge(l1_step, 4)
            dve.wait_ge(own_step, 4)
            dve.wait_ge(consts, 3)

            def swap(dst, src):
                for q, r in ((0, 0), (1, 2), (2, 1), (3, 3)):
                    last = dve.transpose(dst[32 * r:32 * r + 32, :], src[32 * q:32 * q + 32, :])
                return last

            with dve.Fori(0, B) as b:
                def split_next(s):
                    if s < SPLITS and not by_pool(s):
                        split_low(dve, b, s)

                def step(n):
                    dve.wait_ge(stat, b * STATS + n)

                for s in range(AHEAD):
                    split_next(s)
                for i in range(UNITS):
                    split_next(2 * i + AHEAD)
                    split_next(2 * i + AHEAD + 1)
                    dve.wait_ge(qk_hi, b * UNITS + i + 1)
                    for lo, dst, high in ((0, q_parts[64:128], q_parts[0:64]), (64, k_low[64:128], k_high[64:128])):
                        last = dve.scalar_tensor_tensor(
                            out=unit_pixels(dst, i), in0=ps[lo:lo + 64, QK_BANK + i % 2, :],
                            scalar=bqk_sb[lo:lo + 64, :], in1=unit_pixels(high, i).bitcast(F32),
                            op0=ALU.add, op1=ALU.subtract)
                    last.then_inc(qk_lo, 1)
                for i in range(UNITS):
                    dve.tensor_reduce(amax_u[:, i:i + 1], x_rows(ROWS * i, ROWS), mybir.AxisListType.XY, ALU.max,
                                      apply_absolute_value=True).then_inc(amax_step, 1)
                dve.wait_ge(amax_step, b * (UNITS + 1) + UNITS)
                dve.tensor_reduce(amax_p[:], amax_u[:], AX_X, ALU.max).then_inc(amax_step, 1)
                dve.wait_ge(amax_done, b + 1)
                dve.tensor_scalar(bound[:], amax_all[:], l1_all[:, 0:1], 2.0 ** -90, ALU.mult,
                                  ALU.max).then_inc(scale_step, 1)
                dve.wait_ge(scale_step, b * 4 + 1)
                dve.tensor_scalar(expo[:], bound[:].bitcast(I32), 0x7F800000, None,
                                  ALU.bitwise_and).then_inc(scale_step, 1)
                dve.wait_ge(scale_step, b * 4 + 2)
                dve.tensor_scalar(v_inv[:].bitcast(I32), expo[:], float(-V_EXP * MANT), None, ALU.add)
                dve.tensor_scalar(v_mul[:].bitcast(I32), expo[:], -1.0, float((254 + V_EXP) * MANT), ALU.mult,
                                  ALU.add).then_inc(scale_step, 1)
                dve.wait_ge(scale_step, b * 4 + 3)
                dve.tensor_scalar(out_mul[:], v_inv[:], gsc[:, 0:1], None, ALU.mult).then_inc(scale_step, 1)

                for j in range(SPLITS):
                    for t in (2 * j, 2 * j + 1):
                        dve.wait_ge(v_hi, b * HALF + t + 1)
                        dve.scalar_tensor_tensor(out=v_tile(t)[:, 1, :], in0=ps[:, V_BANK + t % V_BANKS, :],
                                                 scalar=v_mul[:, 0:1], in1=v_tile(t)[:, 0, :], op0=ALU.mult,
                                                 op1=ALU.subtract).then_inc(v_lo, 1)
                    if j == 0:
                        dve.wait_ge(s_out, b * 2 * GROUPS + 2 * GROUPS)
                        dve.tensor_reduce(m_row[:], s_row[:], AX_X, ALU.max).then_inc(stat, 1)
                        dve.copy_predicated(s_col[:], ap(own[:], [(0, HALF), (1, 64)]).bitcast(I32),
                                            ap(neg_inf[:], [(0, HALF), (0, 64)])).then_inc(stat, 1)
                        step(2)
                        dve.tensor_reduce(m_col[:], s_col[:], AX_X, ALU.max).then_inc(stat, 1)
                        step(3)
                        swap(t_row, m_col).then_inc(stat, 1)
                        step(4)
                        dve.tensor_tensor(mj_row[:], m_row[:], t_row[:], ALU.max).then_inc(stat, 1)
                        step(5)
                        swap(mj_col, mj_row).then_inc(stat, 1)
                        step(6)
                    if j in (1, 2):
                        s, m = ((s_row, mj_row), (s_col, mj_col))[j - 1]
                        dve.tensor_tensor(s[:], s[:], over_line(m), ALU.subtract).then_inc(shifted, 1)
                    if j == EXP_AT + 2:
                        dve.wait_ge(exped, b * 2 + 2)
                        dve.tensor_reduce(m_row[:], s_row[:], AX_X, ALU.add)
                        dve.tensor_reduce(m_col[:], s_col[:], AX_X, ALU.add).then_inc(stat, 1)
                        step(7)
                        swap(t_row, m_col).then_inc(stat, 1)
                        step(8)
                        dve.tensor_tensor(mj_row[:], m_row[:], t_row[:], ALU.add).then_inc(stat, 1)
                        step(9)
                        dve.reciprocal(r_row[:], mj_row[:]).then_inc(stat, 1)
                        step(10)
                        dve.tensor_scalar(mj_row[:], r_row[:], P_SCALE, None, ALU.mult).then_inc(stat, 1)
                        step(11)
                        swap(mj_col, mj_row).then_inc(stat, 1)
                        step(12)
                    if j in (EXP_AT + 3, EXP_AT + 4):
                        s, r = ((s_row, mj_row), (s_col, mj_col))[j - EXP_AT - 3]
                        dve.tensor_tensor(s[:], s[:], over_line(r), ALU.mult).then_inc(probs, 1)

                dve.wait_ge(biased, b * UNITS + UNITS)
                dve.wait_ge(scale_step, b * 4 + 4)
                for g, (kind, n) in enumerate(APPLY):
                    for k in range(SET):
                        t, i = SET * n + k, SET * g + k
                        if i in (COL_FROM, COL_TO):
                            dve.wait_ge(added, b * TILES + i)
                        dve.wait_ge(out_mm, b * TILES + i + 1)
                        bank = ps[:, OUT_BANK + i % 4, :]
                        sums, place = sums_and_place(kind, t, bank)
                        dve.scalar_tensor_tensor(out=place, in0=sums, scalar=out_mul[:, 0:1], in1=place,
                                                 op0=ALU.mult, op1=ALU.add).then_inc(added, 1)

        @block.gpsimd
        def _(pool):
            pool.memset(ident[:], 0.0).then_inc(ident_zero, 1)
            pool.memset(zero[:], 0.0).then_inc(ident_zero, 1)
            pool.memset(own[:], 0.0).then_inc(ident_zero, 1)
            pool.wait_ge(ident_zero, 3)
            pool.affine_select(out=ident[:], in_=ident[:], compare_op=ALU.not_equal, fill=1.0, base=0,
                               pattern=[[-1, P]], channel_multiplier=1).then_inc(ident_made, 1)
            pool.wait_ge(ident_made, 1)
            for q in range(4):
                if q:
                    pool.wait_ge(own_step, q)
                part = own[32 * q:32 * q + 32, :]
                pool.affine_select(out=part, in_=part, compare_op=ALU.not_equal, fill=1.0, base=q % 2,
                                   pattern=[[-1, 64]], channel_multiplier=2).then_inc(own_step, 1)
            pool.wait_ge(own_step, 4)
            pool.wait_ge(l1_step, 2)
            pool.partition_all_reduce(l1_all[:], l1p[:], P, RMAX).then_inc(l1_step, 1)

            def wait(semaphore, value, n):
                pool.wait_ge(semaphore, value)
                pool.tensor_tensor(tick[:, n:n + 1], zero[:], zero[:], ALU.add)

            with pool.Fori(0, B) as b:
                def split_next(s):
                    if by_pool(s) and s < SPLITS + 2:
                        split_low(pool, b, s)

                for s in range(AHEAD):
                    split_next(s)
                for i in range(UNITS):
                    split_next(2 * i + AHEAD)
                    split_next(2 * i + AHEAD + 1)
                    pool.wait_ge(qk_lo, b * UNITS + i + 1)
                    for a in range(2):
                        src = ap(q_parts[:, ROWS * P * i + W * a:ROWS * P * i + W * a + 1],
                                 [(P, ROWS), (HALF, 2), (1, HALF)]).bitcast(F32)
                        dst = ap(q_cols[:, 0, HALF * a + ROWS * i:HALF * a + ROWS * i + 1],
                                 [(1, ROWS), (64, 2), (P, HALF)])
                        last = pool.tensor_tensor(dst, src, ap(zero[:], [(0, ROWS), (0, 2), (0, HALF)]), ALU.add)
                    last.then_inc(q_turned, 1)
                for j in range(2, EARLY):
                    split_low(pool, b, SPLITS + j)
                wait(amax_step, b * (UNITS + 1) + UNITS + 1, 0)
                pool.partition_all_reduce(amax_all[:], amax_p[:], P, RMAX).then_inc(amax_done, 1)
                for j in range(EARLY, SPLITS):
                    split_low(pool, b, SPLITS + j)
                for g in range(len(APPLY)):
                    pool.wait_ge(pt_hi, b * len(APPLY) + g + 1)
                    pool.wait_ge(pt_out, b * len(APPLY) + g + 1)
                    for a in range(2):
                        half = slice(64 * a, 64 * a + 64)
                        high, low = (pt[half, g % 2, part, :, half] for part in range(2))
                        last = pool.tensor_tensor(low, pt_whole[half, g % 2], high, ALU.subtract)
                    last.then_inc(pt_lo, 1)


_OUT = ((16, 512, 64, 64), "float32")


def kernel(x, L0_conv_Wq, L0_conv_bq, L0_conv_Wk, L0_conv_bk, L0_conv_Wv, L0_conv_bv, L0_conv_gamma):
    import numpy as np
    import concourse.bacc as bacc
    from concourse.bass_utils import run_bass_kernel_spmd

    nc = bacc.Bacc("TRN2", target_bir_lowering=False, num_devices=1)
    wq, wk, wv = (np.asarray(w) for w in (L0_conv_Wq, L0_conv_Wk, L0_conv_Wv))
    given = {
        "x": np.asarray(x),
        "wqk_t": np.concatenate([wq.T, wk.T], axis=1),
        "bqk": np.concatenate([np.asarray(L0_conv_bq), np.asarray(L0_conv_bk)]).reshape(-1, 1),
        "wv_t": wv.T,
        "wv": wv,
        "bv": np.asarray(L0_conv_bv).reshape(-1, 128).T,
        "gamma": np.broadcast_to(np.asarray(L0_conv_gamma).reshape(1, 1), (128, 1)),
    }
    arrays = {f"{name}_dram": np.ascontiguousarray(a) for name, a in given.items()}
    args = [nc.dram_tensor(name, a.shape, mybir.dt.from_np(a.dtype), kind="ExternalInput").ap()
            for name, a in arrays.items()]
    shape, dtype = _OUT
    args.append(nc.dram_tensor("out_dram", shape, mybir.dt.from_np(np.dtype(dtype)), kind="ExternalOutput").ap())
    criss_cross(nc, *args)
    return run_bass_kernel_spmd(nc, [arrays], core_ids=[0]).results[0]["out_dram"]
```

```python
from contextlib import ExitStack

import concourse.bass as bass
from concourse import mybir

ALU = mybir.AluOpType
ACT = mybir.ActivationFunctionType
F32 = mybir.dt.float32
F32R = mybir.dt.float32r
F16 = mybir.dt.float16
I32 = mybir.dt.int32
AX_X = mybir.AxisListType.X
RMAX = bass.bass_isa.ReduceOp.max

P = 128
NEG_INF = -1e30
P_SCALE = 2.0 ** 12
V_EXP = 14
MANT = 1 << 23


def criss_cross(nc, x, wqk_t, bqk, wv_t, wv, bv, gamma, out):
    B, C, H, W = x.shape
    CH = C // P
    CQ = wqk_t.shape[1] // 2
    HALF = H // 2
    PIX = H * W
    assert CQ == 64 and H == W == 64 and C == CH * P and bqk.shape[0] == P
    UNITS = 8
    ROWS = HALF // UNITS
    SPLITS = HALF // 2
    GROUPS = HALF // 4
    SET = 8
    SETS = HALF // SET
    APPLY = [("row", g) for g in range(SETS)] + [("col", g) for g in range(SETS)]
    TILES = SET * len(APPLY)
    COL_FROM = HALF
    QUARTER = H // 4
    EXP_AT = 5
    EARLY = 2
    ALL_SPLITS = 2 * SPLITS - EARLY // 2
    QK_SLOTS = 4
    RING = 4
    BEHIND_V = [("col", 0), ("x", 0), ("col", 1), ("x", 1), ("col", 2), ("x", 2), ("col", 3), ("x", 3), ("x", 4)] + \
        [("col", n) for n in range(RING, HALF // 2)] + [("x", 5), ("x", 6)]
    STORES = [(0, 0), (1, 0), (2, 0), (2, 1), (2, 2), (2, 3), (0, 1), (1, 1), ("x", 7)] + \
        [(0, 2), (1, 2), (0, 3), (1, 3)] + [(3, q) for q in range(4)]
    POOL_QK = (0, 2, 5, 8, 11, 14)
    AHEAD = 3
    SETS_AT = (24, 28)
    TURN_LATE = 1
    EARLY_AMAX = 1
    STATS = 12
    PITCH = W + 2

    v_dram = nc.dram_tensor("v_dram", (H, PITCH, 2 * C), F16, kind="Internal").ap()

    with ExitStack() as ctx:
        def sb(name, shape, dt):
            return ctx.enter_context(nc.sbuf_tensor(name, shape, dt))

        def sem(name):
            return ctx.enter_context(nc.semaphore(name))

        wv_hi = sb("wv_hi", [P, CH, C], F32R)
        wv_lo = sb("wv_lo", [P, CH, C], F32R)
        wqk_hi = sb("wqk_hi", [P, CH, P], F32R)
        wqk_lo = sb("wqk_lo", [P, CH, P], F32R)
        split_lo = sb("split_lo", [P, 2, 2, CH, P], F32R)
        pt = sb("pt", [P, 2, 2, SET, P], F16)
        ident = sb("ident", [P, P], F32)
        own = sb("own", [P, 64], F32)
        neg_inf = sb("neg_inf", [P, 1], F32)
        zero = sb("zero", [P, 1], F32)
        tick = sb("tick", [P, 16], F32)
        bqk_sb = sb("bqk_sb", [P, 1], F32)
        gamma_sb = sb("gamma_sb", [P, 1], F32)
        bv_sb = sb("bv_sb", [P, CH], F32)
        gbv = sb("gbv", [P, CH], F32)
        gsc = sb("gsc", [P, 1], F32)
        l1 = sb("l1", [P, CH], F32)
        l1p = sb("l1p", [P, 1], F32)
        l1_all = sb("l1_all", [P, 1], F32)
        amax_u = sb("amax_u", [P, UNITS], F32)
        amax_p = sb("amax_p", [P, 1], F32)
        amax_all = sb("amax_all", [P, 1], F32)
        bound = sb("bound", [P, 1], F32)
        expo = sb("expo", [P, 1], I32)
        v_mul = sb("v_mul", [P, 1], F32)
        v_inv = sb("v_inv", [P, 1], F32)
        out_mul = sb("out_mul", [P, 1], F32)
        m_row = sb("m_row", [P, HALF], F32)
        m_col = sb("m_col", [P, HALF], F32)
        t_row = sb("t_row", [P, HALF], F32)
        mj_row = sb("mj_row", [P, HALF], F32)
        mj_col = sb("mj_col", [P, HALF], F32)
        r_row = sb("r_row", [P, HALF], F32)

        def shared(*tensors):
            made = []
            for name, shape, dt in tensors[:-1]:
                with nc.sbuf_tensor(name, shape, dt) as t:
                    made.append(t)
            name, shape, dt = tensors[-1]
            return made + [sb(name, shape, dt)]

        pt_whole, split_hi = shared(("pt_whole", [P, 2, SET, 64], F32), ("split_hi", [P, 2, 2, CH, P], F32R))
        pt_first, q_parts, v_ring = shared(("pt_first", [P, 2, SET, 64], F32), ("q_parts", [P, PIX], F32R),
                                           ("v_ring", [P, RING, 2, CH, 2 * P], F16))
        more_hi, s_row = shared(("more_hi", [P, 2, 2, CH, P], F32R), ("s_row", [P, HALF, 64], F32))
        more_lo, s_col = shared(("more_lo", [P, 2, 2, CH, P], F32R), ("s_col", [P, HALF, 64], F32))

        with nc.sbuf_tensor("before_weights", [P, CH * PIX - 2 * CH * C - CH * P], F32), \
                nc.sbuf_tensor("wqk_sb", [P, CH, P], F32) as wqk_sb, \
                nc.sbuf_tensor("wv_t_sb", [P, CH, C], F32) as wv_t_sb, \
                nc.sbuf_tensor("wv_sb", [P, CH, C], F32) as wv_sb:
            pass
        xs, v_rows, k_high, k_low, q_cols = [None] * 2, [None] * 2, [None] * 2, [None] * 2, [None] * 2
        for region in (1, 0):
            m = 1 - region
            with nc.sbuf_tensor(f"k_high{m}", [P, PIX], F32R) as k_high[m], \
                    nc.sbuf_tensor(f"k_low{m}", [P, PIX], F32R) as k_low[m], \
                    nc.sbuf_tensor(f"q_cols{m}", [P, HALF, P], F32R) as q_cols[m]:
                pass
            v_rows[m], xs[region] = shared((f"v_rows{m}", [P, CH, H, 2 * W], F16),
                                           (f"xs{region}", [P, CH, H, W], F32))

        def v_tile(m, t):
            row = HALF * (t % 2) + t - t % 2
            return ap(v_rows[m][:, 0, row, :], [(2 * H * W, CH), (1, 2 * P)])

        ps = ctx.enter_context(nc.psum_tensor("ps", [P, 8, 512], F32))
        S_BANK, V_BANK, QK_BANK, PT_BANK = 0, 4, 6, 4
        V_BANKS = 4
        OUT_BANKS = (0, 1, 2, 3, 6, 7)
        OUTS = len(OUT_BANKS)

        w_loaded = sem("w_loaded")
        w_rest_loaded = sem("w_rest_loaded")
        w_split = sem("w_split")
        consts = sem("consts")
        ident_zero = sem("ident_zero")
        ident_made = sem("ident_made")
        own_step = sem("own_step")
        l1_step = sem("l1_step")
        x_loaded = [sem(f"x_loaded{i}") for i in range(UNITS)]
        stored = [[sem(f"stored{c}{q}") for q in range(4)] for c in range(2)] + \
            [[sem(f"stored{c}")] * 4 for c in range(2, CH)]
        hi_split = sem("hi_split")
        lo_split = sem("lo_split")
        lo_split_pool = sem("lo_split_pool")
        qk_mm = sem("qk_mm")
        qk_hi = sem("qk_hi")
        qk_lo = sem("qk_lo")
        k_copied = [sem(f"k_copied{i}") for i in range(UNITS)]
        q_turned = sem("q_turned")
        s_mm = sem("s_mm")
        s_out = sem("s_out")
        amax_step = sem("amax_step")
        amax_done = sem("amax_done")
        stat = sem("stat")
        scale_step = sem("scale_step")
        shifted = sem("shifted")
        exped = sem("exped")
        probs = sem("probs")
        v_mm = sem("v_mm")
        v_hi = sem("v_hi")
        v_lo = sem("v_lo")
        v_stored = sem("v_stored")
        col_loaded = [sem(f"col_loaded{i}") for i in range(RING)]
        biased = sem("biased")
        pt_mm = sem("pt_mm")
        pt_out = sem("pt_out")
        pt_hi = sem("pt_hi")
        pt_lo = sem("pt_lo")
        out_mm = sem("out_mm")
        added = sem("added")

        def ap(base, dims):
            return bass.AP(base.tensor, base.offset, [base.ap[0], *[list(d) for d in dims]])

        def x_rows(m, r, n):
            return ap(xs[m][:, 0, r, :], [(HALF * W, 2 * CH), (1, n * W)])

        def x_tiles(m, j):
            return ap(xs[m][:, 0, 2 * j, :], [(W, 2), (HALF * W, 2 * CH), (1, W)])

        def rows_of(s):
            return s if s < SPLITS else s - SPLITS + EARLY // 2

        def split_for_v(t):
            return 0 if t < EARLY else SPLITS + (t - EARLY) // 2

        def slot(part, s):
            if s < SPLITS and s % QK_SLOTS >= 2:
                return {"hi": more_hi, "lo": more_lo}[part][:, s % 2]
            return {"hi": split_hi, "lo": split_lo}[part][:, rows_of(s) % 2]

        def by_row(split):
            return split.rearrange("p r c (a w) -> p r (c a) w", a=2)

        def unit_pixels(part, i):
            return part[:, ROWS * P * i:ROWS * P * (i + 1)]

        def col_keys(t, part):
            return ap(part[:, t:t + 1], [(HALF, 2), (1, 2), (W, H)])

        def unit_pairs(t, b, m, i):
            chans = t[b].rearrange("(c p) h w -> p c h w", p=P)
            rows = [slice(a * HALF + ROWS * i, a * HALF + ROWS * (i + 1)) for a in range(2)]
            return [(chans[:, :, r, :].rearrange("p c h w -> p c (h w)"),
                     xs[m][:, :, r, :].rearrange("p c h w -> p c (h w)")) for r in rows]

        def over_line(stats):
            return stats[:].unsqueeze(2).to_broadcast([P, HALF, 64])

        def v_bank(t):
            return ps[:, V_BANK + t % V_BANKS, :].rearrange("p (c n) -> p c n", n=P)

        def pt_bank(g):
            return S_BANK + g if g < 2 else PT_BANK + g % 2

        def transposed(g, a, k):
            pairs = ps[64 * k:64 * k + 64, pt_bank(g), :].rearrange("p (i n) -> p i n", n=P)
            return pairs[:, :, 64 * a:64 * a + 64]

        def placed(g, part, a, k):
            pairs = pt[64 * a:64 * a + 64, g % 2, part].rearrange("p (i k) n -> p i k n", k=2)
            return pairs[:, :, k, 64 * a:64 * a + 64]

        def whole(g):
            return pt_first[:, g] if g < 2 else pt_whole[:, g % 2]

        def placed_whole(g, a, k):
            return whole(g)[64 * a:64 * a + 64].rearrange("p (i k) n -> p i k n", k=2)[:, :, k]

        def by_pool(s):
            return s >= SPLITS or s in POOL_QK

        DVE_SPLITS = sum(not by_pool(s) for s in range(ALL_SPLITS))

        def wait_lo_split(eng, b, s):
            if by_pool(s):
                n = sum(by_pool(r) for r in range(s + 1))
                eng.wait_ge(lo_split_pool, b * (ALL_SPLITS - DVE_SPLITS) + n)
            else:
                n = sum(not by_pool(r) for r in range(s + 1))
                eng.wait_ge(lo_split, b * DVE_SPLITS + n)

        def sums_and_place(m, kind, t, sums):
            if kind == "row":
                return sums.rearrange("p (c n) -> p c n", n=W), x_rows(m, t, 1)
            return sums.rearrange("p (a n) -> p a n", a=2), ap(xs[m][:, 0, 0, t:t + 1], [(HALF, 2), (W, CH * H)])

        def split_low(eng, b, m, s):
            eng.wait_ge(hi_split, b * ALL_SPLITS + s + 1)
            if s < SPLITS:
                eng.wait_ge(x_loaded[s // 2], b * 32 + 32)
            slot_free(eng, b, s)
            eng.tensor_tensor(by_row(slot("lo", s)), x_tiles(m, rows_of(s)), by_row(slot("hi", s)).bitcast(F32),
                              ALU.subtract).then_inc(lo_split_pool if by_pool(s) else lo_split, 1)

        def slot_free(eng, b, s):
            if s < QK_SLOTS:
                return
            j = rows_of(s)
            if s == QK_SLOTS:
                eng.wait_ge(v_mm, b * HALF + EARLY)
            elif s < SPLITS:
                eng.wait_ge(qk_mm, b * SPLITS + s - QK_SLOTS + 1)
            elif j <= 2:
                eng.wait_ge(qk_mm, b * SPLITS + SPLITS - QK_SLOTS + j % 2 + 1)
            else:
                eng.wait_ge(v_mm, b * HALF + 2 * j - 2)

        block = ctx.enter_context(nc.Block())

        @block.sync
        def _(sp):
            def load(b, m, i):
                for src, dst in unit_pairs(x, b, m, i):
                    sp.dma_start(dst, src).then_inc(x_loaded[i], 16)

            sp.dma_start(wqk_sb[:], wqk_t.rearrange("(c p) n -> p c n", p=P)).then_inc(w_loaded, 16)
            sp.dma_start(bqk_sb[:], bqk).then_inc(w_loaded, 16)
            sp.dma_start(wv_t_sb[:], wv_t.rearrange("(c p) n -> p c n", p=P)).then_inc(w_loaded, 16)
            load(0, 0, 0)
            sp.dma_start(gamma_sb[:], gamma).then_inc(w_rest_loaded, 16)
            sp.dma_start(bv_sb[:], bv).then_inc(w_rest_loaded, 16)
            sp.dma_start(wv_sb[:], wv.rearrange("(c p) n -> p c n", p=P)).then_inc(w_rest_loaded, 16)
            for i in range(1, UNITS):
                load(0, 0, i)

            def column_tiles(b, n):
                if n >= RING:
                    sp.wait_ge(out_mm, b * TILES + COL_FROM + 2 * (n - RING) + 2)
                for a in range(2):
                    sp.dma_start(
                        v_ring[64 * a:64 * a + 64, n % RING].rearrange("p t c s -> p (t c s)"),
                        v_dram[:, a * HALF + 2 * n:a * HALF + 2 * n + 2, :].rearrange("h t c -> h (t c)"),
                    ).then_inc(col_loaded[n % RING], 16)

            def next_unit(b, m, i):
                sp.wait_ge(out_mm, b * TILES + ROWS * (i + 1))
                load(b + 1, 1 - m, i)

            def store(b, m, c, q):
                rows = slice(QUARTER * q, QUARTER * (q + 1))
                chans = out[b].rearrange("(c p) h w -> c p h w", p=P)
                sp.dma_start(chans[c, :, rows, :].rearrange("p h w -> p (h w)"),
                             xs[m][:, c, rows, :].rearrange("p h w -> p (h w)")).then_inc(stored[c][q], 16)

            def image(b, m, following):
                for t in range(HALF):
                    sp.wait_ge(v_hi, b * HALF + t + 1)
                    sp.wait_ge(v_lo, b * HALF + t + 1)
                    for a in range(2):
                        sp.dma_start(v_dram[2 * t + a, 0:W, :].rearrange("w (c s) -> w c s", c=CH),
                                     v_tile(m, t)[64 * a:64 * a + 64]).then_inc(v_stored, 16)
                sp.wait_ge(v_stored, b * (HALF * 32) + HALF * 32)
                sp.wait_ge(pt_lo, b * len(APPLY) + 2)
                for what, n in BEHIND_V:
                    if what == "col":
                        column_tiles(b, n)
                    elif following:
                        next_unit(b, m, n)
                sp.wait_ge(added, b * TILES + TILES)
                for what, n in STORES:
                    if what == "x" and following:
                        next_unit(b, m, n)
                    elif what != "x":
                        store(b, m, what, n)

            if B > 2:
                with sp.Fori(0, B - 2, 2) as b:
                    for m in range(2):
                        image(b + m, m, True)
            image(B - 2, 0, True)
            image(B - 1, 1, False)
            for c, q in [(c, q) for c in range(2) for q in range(4)]:
                sp.wait_ge(stored[c][q], 16 * B + 16)
            for c in range(2, CH):
                sp.wait_ge(stored[c][0], 64 * B + 16)

        @block.tensor
        def _(pe):
            pe.wait_ge(w_split, 4)
            pe.wait_ge(consts, 3)
            pe.wait_ge(ident_made, 1)

            def products(dst, chunks):
                for c, (lh, ll, rh, rl) in enumerate(chunks):
                    pe.matmul(dst, lh, rh, start=(c == 0), stop=False)
                    pe.matmul(dst, lh, rl, start=False, stop=False)
                    last = pe.matmul(dst, ll, rh, start=False, stop=(c == CH - 1))
                return last

            def split_ready(b, s):
                pe.wait_ge(hi_split, b * ALL_SPLITS + s + 1)
                wait_lo_split(pe, b, s)

            def v_tiles(b, start, end):
                for t in range(start, end):
                    hi, lo = (slot(part, split_for_v(t))[:, t % 2] for part in ("hi", "lo"))
                    if t % 2 == 0:
                        split_ready(b, split_for_v(t))
                    if t >= V_BANKS:
                        pe.wait_ge(v_lo, b * HALF + t - V_BANKS + 1)
                    elif t >= V_BANKS - 2:
                        pe.wait_ge(qk_lo, b * UNITS + UNITS - (V_BANKS - 1 - t))
                    last = products(ps[:, V_BANK + t % V_BANKS, :],
                                    [(hi[:, c], lo[:, c], wv_hi[:, c], wv_lo[:, c]) for c in range(CH)])
                    last.then_inc(v_mm, 1)

            def image(b, m):
                for s in range(SPLITS):
                    if s % 2 == 0 and s >= 4:
                        pe.wait_ge(qk_lo, b * UNITS + s // 2 - 1)
                    split_ready(b, s)
                    dst = ps[:, QK_BANK + s // 2 % 2, 256 * (s % 2):256 * (s % 2) + 256]
                    hi, lo = slot("hi", s), slot("lo", s)
                    products(dst, [(wqk_hi[:, c], wqk_lo[:, c], hi[:, :, c], lo[:, :, c])
                                   for c in range(CH)]).then_inc(qk_mm, 1)
                    if s == 0:
                        v_tiles(b, 0, EARLY)
                for n in range(2 * GROUPS):
                    if n < GROUPS:
                        pe.wait_ge(qk_lo, b * UNITS + n + 1)
                        pe.wait_ge(k_copied[n], b * 32 + 32)
                    elif n == GROUPS:
                        pe.wait_ge(q_turned, b * UNITS + UNITS)
                    if n >= 2:
                        pe.wait_ge(s_out, b * 2 * GROUPS + n - 1)
                    for k in range(4):
                        t = 4 * (n % GROUPS) + k
                        dst = ps[:, S_BANK + 2 * (n % 2) + k // 2, 256 * (k % 2):256 * (k % 2) + 256]
                        pair = t - k % 2
                        if n < GROUPS:
                            queries = q_parts[:, P * t:P * t + P]
                            keys = [part[:, P * pair:P * pair + 2 * P] for part in (k_high[m], k_low[m])]
                        else:
                            queries = q_cols[m][:, t]
                            keys = [col_keys(pair, part) for part in (k_high[m], k_low[m])]
                        pe.matmul(dst, queries, keys[0], start=True, stop=False)
                        last = pe.matmul(dst, queries, keys[1], start=False, stop=True)
                    last.then_inc(s_mm, 1)
                def transposes(g):
                    kind, n = APPLY[g]
                    src = s_row if kind == "row" else s_col
                    if g in (2, 3):
                        pe.wait_ge(v_lo, b * HALF + HALF - V_BANKS + g % 2 + 1)
                    for k in range(SET // 2):
                        t = SET * n + 2 * k
                        last = pe.transpose(ps[:, pt_bank(g), P * k:P * k + P],
                                            src[:, t:t + 2, :].rearrange("p k u -> p (k u)"), ident[:])
                    last.then_inc(pt_mm, 1)

                v_tiles(b, EARLY, SETS_AT[0])
                pe.wait_ge(probs, b * 2 + 1)
                transposes(0)
                v_tiles(b, *SETS_AT)
                transposes(1)
                v_tiles(b, SETS_AT[1], HALF)
                pe.wait_ge(probs, b * 2 + 2)
                for g, (kind, n) in enumerate(APPLY):
                    if 2 <= g + 1 < len(APPLY):
                        transposes(g + 1)
                    pe.wait_ge(pt_hi, b * len(APPLY) + g + 1)
                    pe.wait_ge(pt_lo, b * len(APPLY) + g + 1)
                    for k in range(SET):
                        t, i = SET * n + k, SET * g + k
                        if i >= OUTS:
                            pe.wait_ge(added, b * TILES + i - OUTS + 1)
                        elif i == 1:
                            pe.wait_ge(pt_out, b * len(APPLY) + 2)
                        elif i in (4, 5):
                            pe.wait_ge(v_lo, b * HALF + HALF - 5 + i)
                        if kind == "row":
                            v = v_tile(m, t)
                        else:
                            turn, place = divmod(t // 2, RING)
                            if t % 2 == 0:
                                pe.wait_ge(col_loaded[place], b * (HALF // 2 // RING * 32) + (turn + 1) * 32)
                            v = v_ring[:, place, t % 2]
                        for c in range(CH):
                            if kind == "row":
                                dst = ps[:, OUT_BANKS[i % OUTS], P * c:P * c + P]
                            else:
                                dst = ap(ps[:, OUT_BANKS[i % OUTS], 64 * c:64 * c + 1], [(256, 2), (1, 64)])
                            v_high_part, v_low_part = (v[:, c, P * part:P * part + P] for part in range(2))
                            p_high, p_low = (pt[:, g % 2, part, k] for part in range(2))
                            pe.matmul(dst, v_high_part, p_high, start=True, stop=False)
                            pe.matmul(dst, v_high_part, p_low, start=False, stop=False)
                            last = pe.matmul(dst, v_low_part, p_high, start=False, stop=True)
                        last.then_inc(out_mm, 1)
                pe.wait_ge(added, b * TILES + TILES - 4)

            with pe.Fori(0, B, 2) as b:
                for m in range(2):
                    image(b + m, m)

        @block.scalar
        def _(act):
            act.wait_ge(w_loaded, 16 * 3)
            act.activation(wqk_hi[:], wqk_sb[:], ACT.Copy).then_inc(w_split, 1)
            act.activation(wv_hi[:], wv_t_sb[:], ACT.Copy).then_inc(w_split, 1)

            def split(b, m, s):
                if s < SPLITS and s % 2 == 0:
                    act.wait_ge(x_loaded[s // 2], b * 32 + 32)
                slot_free(act, b, s)
                act.activation(by_row(slot("hi", s)), x_tiles(m, rows_of(s)), ACT.Copy).then_inc(hi_split, 1)

            def image(b, m):
                def copy_k(i):
                    for part, made in ((k_high[m], qk_hi), (k_low[m], qk_lo)):
                        act.wait_ge(made, b * UNITS + i + 1)
                        act.dma_start(unit_pixels(part[0:64], i).bitcast(F32),
                                      unit_pixels(part[64:128], i).bitcast(F32)).then_inc(k_copied[i], 16)

                for s in range(AHEAD):
                    split(b, m, s)
                for i in range(UNITS):
                    for s in (2 * i + AHEAD, 2 * i + AHEAD + 1):
                        if s < SPLITS + 2:
                            split(b, m, s)
                    act.wait_ge(qk_mm, b * SPLITS + 2 * i + 2)
                    if i % 2 == 0:
                        act.wait_ge(stored[0][i // 2], b * 16 + 16)
                    for lo, part in ((0, q_parts), (64, k_high[m])):
                        last = act.activation(unit_pixels(part[lo:lo + 64], i), ps[lo:lo + 64, QK_BANK + i % 2, :],
                                              ACT.Identity, bias=bqk_sb[lo:lo + 64, :])
                    last.then_inc(qk_hi, 1)
                    if i:
                        copy_k(i - 1)
                for n in range(2 * GROUPS):
                    act.wait_ge(s_mm, b * 2 * GROUPS + n + 1)
                    dst = s_row if n < GROUPS else s_col
                    tile_step, half_step = (P, 64) if n < GROUPS else (64, P)
                    for a in range(2):
                        src = ap(ps[64 * a:64 * a + 64, S_BANK + 2 * (n % 2), half_step * a:half_step * a + 1],
                                 [(512, 2), (256 + tile_step, 2), (1, 64)])
                        t = 4 * (n % GROUPS)
                        last = act.activation(
                            dst[64 * a:64 * a + 64, t:t + 4, :].rearrange("p (i k) u -> p i k u", i=2), src, ACT.Copy)
                    last.then_inc(s_out, 1)
                    if n == 1:
                        copy_k(UNITS - 1)
                def probabilities_out(g):
                    act.wait_ge(pt_mm, b * len(APPLY) + g + 1)
                    if g >= 2:
                        act.wait_ge(out_mm, b * TILES + SET * (g - 1))
                        act.wait_ge(pt_lo, b * len(APPLY) + g - 1)
                    for semaphore, dst in ((pt_hi, lambda a, k: placed(g, 0, a, k)),
                                           (pt_out, lambda a, k: placed_whole(g, a, k))):
                        for k in range(2):
                            for a in range(2):
                                last = act.activation(dst(a, k), transposed(g, a, k), ACT.Copy)
                        last.then_inc(semaphore, 1)

                act.wait_ge(scale_step, b * 4 + 3)
                act.wait_ge(stored[3][0], b * 64 + 16)
                for j in range(SPLITS):
                    for t in (2 * j, 2 * j + 1):
                        act.wait_ge(v_mm, b * HALF + t + 1)
                        act.activation(v_tile(m, t)[:, :, 0:P], v_bank(t), ACT.Copy,
                                       scale=v_mul[:, 0:1]).then_inc(v_hi, 1)
                    if 1 <= j < SPLITS - 2:
                        split(b, m, split_for_v(2 * j + 4))
                    if 2 * j in SETS_AT:
                        probabilities_out(SETS_AT.index(2 * j))
                    if j % 2 == 1:
                        wait_lo_split(act, b, split_for_v(2 * j))
                        for c in range(CH):
                            place = ap(xs[m][:, c, ROWS * (j // 2), :], [(HALF * W, 2), (1, ROWS * W)])
                            last = act.activation(place, place, ACT.Identity, bias=gbv[:, c:c + 1])
                        last.then_inc(biased, 1)
                    if j in (EXP_AT, EXP_AT + 1):
                        n = j - EXP_AT
                        act.wait_ge(shifted, b * 2 + n + 1)
                        s = (s_row, s_col)[n]
                        act.activation(s[:], s[:], ACT.Exp).then_inc(exped, 1)

                for g in range(2, len(APPLY)):
                    probabilities_out(g)
                act.wait_ge(pt_lo, b * len(APPLY) + len(APPLY))

            with act.Fori(0, B, 2) as b:
                for m in range(2):
                    image(b + m, m)

        @block.vector
        def _(dve):
            dve.memset(pt[:], 0.0).then_inc(consts, 1)
            dve.memset(neg_inf[:], NEG_INF).then_inc(consts, 1)
            dve.wait_ge(w_loaded, 16 * 3)
            dve.wait_ge(w_split, 2)
            dve.tensor_tensor(wqk_lo[:], wqk_sb[:], wqk_hi[:].bitcast(F32), ALU.subtract).then_inc(w_split, 1)
            dve.tensor_tensor(wv_lo[:], wv_t_sb[:], wv_hi[:].bitcast(F32), ALU.subtract).then_inc(w_split, 1)
            dve.wait_ge(w_rest_loaded, 16 * 3)
            dve.tensor_reduce(l1[:], wv_sb[:], AX_X, ALU.add, apply_absolute_value=True).then_inc(l1_step, 1)
            dve.wait_ge(l1_step, 1)
            dve.tensor_reduce(l1p[:], l1[:], AX_X, ALU.max).then_inc(l1_step, 1)
            dve.tensor_scalar(gbv[:], bv_sb[:], gamma_sb[:, 0:1], None, ALU.mult).then_inc(consts, 1)
            dve.tensor_scalar(gsc[:], gamma_sb[:], 1.0 / P_SCALE, None, ALU.mult).then_inc(l1_step, 1)
            dve.wait_ge(l1_step, 4)
            dve.wait_ge(own_step, 4)
            dve.wait_ge(consts, 3)

            def swap(dst, src):
                for q, r in ((0, 0), (1, 2), (2, 1), (3, 3)):
                    last = dve.transpose(dst[32 * r:32 * r + 32, :], src[32 * q:32 * q + 32, :])
                return last

            def image(b, m):
                def split_next(s):
                    if s < SPLITS and not by_pool(s):
                        split_low(dve, b, m, s)

                def step(n):
                    dve.wait_ge(stat, b * STATS + n)

                def amax_of_unit(i):
                    dve.wait_ge(x_loaded[i], b * 32 + 32)
                    dve.tensor_reduce(amax_u[:, i:i + 1], x_rows(m, ROWS * i, ROWS), mybir.AxisListType.XY, ALU.max,
                                      apply_absolute_value=True).then_inc(amax_step, 1)

                for s in range(AHEAD):
                    split_next(s)
                for i in range(UNITS):
                    split_next(2 * i + AHEAD)
                    split_next(2 * i + AHEAD + 1)
                    if i % 2 == 0:
                        dve.wait_ge(stored[1][i // 2], b * 16 + 16)
                    dve.wait_ge(qk_hi, b * UNITS + i + 1)
                    for lo, dst, high in ((0, q_parts[64:128], q_parts[0:64]),
                                          (64, k_low[m][64:128], k_high[m][64:128])):
                        last = dve.scalar_tensor_tensor(
                            out=unit_pixels(dst, i), in0=ps[lo:lo + 64, QK_BANK + i % 2, :],
                            scalar=bqk_sb[lo:lo + 64, :], in1=unit_pixels(high, i).bitcast(F32),
                            op0=ALU.add, op1=ALU.subtract)
                    last.then_inc(qk_lo, 1)
                    if i < EARLY_AMAX:
                        amax_of_unit(i)
                for i in range(EARLY_AMAX, UNITS):
                    amax_of_unit(i)
                dve.wait_ge(amax_step, b * (UNITS + 1) + UNITS)
                dve.tensor_reduce(amax_p[:], amax_u[:], AX_X, ALU.max).then_inc(amax_step, 1)
                dve.wait_ge(amax_done, b + 1)
                dve.tensor_scalar(bound[:], amax_all[:], l1_all[:, 0:1], 2.0 ** -90, ALU.mult,
                                  ALU.max).then_inc(scale_step, 1)
                dve.wait_ge(scale_step, b * 4 + 1)
                dve.tensor_scalar(expo[:], bound[:].bitcast(I32), 0x7F800000, None,
                                  ALU.bitwise_and).then_inc(scale_step, 1)
                dve.wait_ge(scale_step, b * 4 + 2)
                dve.tensor_scalar(v_inv[:].bitcast(I32), expo[:], float(-V_EXP * MANT), None, ALU.add)
                dve.tensor_scalar(v_mul[:].bitcast(I32), expo[:], -1.0, float((254 + V_EXP) * MANT), ALU.mult,
                                  ALU.add).then_inc(scale_step, 1)
                dve.wait_ge(scale_step, b * 4 + 3)
                dve.tensor_scalar(out_mul[:], v_inv[:], gsc[:, 0:1], None, ALU.mult).then_inc(scale_step, 1)

                for j in range(SPLITS):
                    for t in (2 * j, 2 * j + 1):
                        if t == 0:
                            dve.wait_ge(s_out, b * 2 * GROUPS + 2 * GROUPS)
                        dve.wait_ge(v_hi, b * HALF + t + 1)
                        dve.scalar_tensor_tensor(out=v_tile(m, t)[:, :, P:2 * P], in0=v_bank(t),
                                                 scalar=v_mul[:, 0:1], in1=v_tile(m, t)[:, :, 0:P], op0=ALU.mult,
                                                 op1=ALU.subtract).then_inc(v_lo, 1)
                    if j == 0:
                        dve.tensor_reduce(m_row[:], s_row[:], AX_X, ALU.max).then_inc(stat, 1)
                    if j == 1:
                        dve.copy_predicated(s_col[:], ap(own[:], [(0, HALF), (1, 64)]).bitcast(I32),
                                            ap(neg_inf[:], [(0, HALF), (0, 64)])).then_inc(stat, 1)
                    if j == 2:
                        step(2)
                        dve.tensor_reduce(m_col[:], s_col[:], AX_X, ALU.max).then_inc(stat, 1)
                        step(3)
                        swap(t_row, m_col).then_inc(stat, 1)
                        step(4)
                        dve.tensor_tensor(mj_row[:], m_row[:], t_row[:], ALU.max).then_inc(stat, 1)
                        step(5)
                        swap(mj_col, mj_row).then_inc(stat, 1)
                        step(6)
                    if j in (3, 4):
                        s, top = ((s_row, mj_row), (s_col, mj_col))[j - 3]
                        dve.tensor_tensor(s[:], s[:], over_line(top), ALU.subtract).then_inc(shifted, 1)
                    if j == EXP_AT + 2:
                        dve.wait_ge(exped, b * 2 + 2)
                        dve.tensor_reduce(m_row[:], s_row[:], AX_X, ALU.add)
                        dve.tensor_reduce(m_col[:], s_col[:], AX_X, ALU.add).then_inc(stat, 1)
                        step(7)
                        swap(t_row, m_col).then_inc(stat, 1)
                        step(8)
                        dve.tensor_tensor(mj_row[:], m_row[:], t_row[:], ALU.add).then_inc(stat, 1)
                        step(9)
                        dve.reciprocal(r_row[:], mj_row[:]).then_inc(stat, 1)
                        step(10)
                        dve.tensor_scalar(mj_row[:], r_row[:], P_SCALE, None, ALU.mult).then_inc(stat, 1)
                        step(11)
                        swap(mj_col, mj_row).then_inc(stat, 1)
                        step(12)
                    if j in (EXP_AT + 3, EXP_AT + 4):
                        s, r = ((s_row, mj_row), (s_col, mj_col))[j - EXP_AT - 3]
                        dve.tensor_tensor(s[:], s[:], over_line(r), ALU.mult).then_inc(probs, 1)

                dve.wait_ge(biased, b * UNITS + UNITS)
                dve.wait_ge(scale_step, b * 4 + 4)
                for g, (kind, n) in enumerate(APPLY):
                    for k in range(SET):
                        t, i = SET * n + k, SET * g + k
                        if i == COL_FROM:
                            dve.wait_ge(added, b * TILES + i)
                        dve.wait_ge(out_mm, b * TILES + i + 1)
                        bank = ps[:, OUT_BANKS[i % OUTS], :]
                        sums, place = sums_and_place(m, kind, t, bank)
                        dve.scalar_tensor_tensor(out=place, in0=sums, scalar=out_mul[:, 0:1], in1=place,
                                                 op0=ALU.mult, op1=ALU.add).then_inc(added, 1)

            with dve.Fori(0, B, 2) as b:
                for m in range(2):
                    image(b + m, m)

        @block.gpsimd
        def _(pool):
            pool.memset(ident[:], 0.0).then_inc(ident_zero, 1)
            pool.memset(zero[:], 0.0).then_inc(ident_zero, 1)
            pool.memset(own[:], 0.0).then_inc(ident_zero, 1)
            for n, semaphore in enumerate(stored[0] + stored[1] + [stored[c][0] for c in range(2, CH)]):
                pool.memset(tick[:, n + 1:n + 2], 0.0).then_inc(semaphore, 16)
            pool.wait_ge(ident_zero, 3)
            pool.affine_select(out=ident[:], in_=ident[:], compare_op=ALU.not_equal, fill=1.0, base=0,
                               pattern=[[-1, P]], channel_multiplier=1).then_inc(ident_made, 1)
            pool.wait_ge(ident_made, 1)
            for q in range(4):
                if q:
                    pool.wait_ge(own_step, q)
                part = own[32 * q:32 * q + 32, :]
                pool.affine_select(out=part, in_=part, compare_op=ALU.not_equal, fill=1.0, base=q % 2,
                                   pattern=[[-1, 64]], channel_multiplier=2).then_inc(own_step, 1)
            pool.wait_ge(own_step, 4)
            pool.wait_ge(l1_step, 2)
            pool.partition_all_reduce(l1_all[:], l1p[:], P, RMAX).then_inc(l1_step, 1)

            def wait(semaphore, value, n):
                pool.wait_ge(semaphore, value)
                pool.tensor_tensor(tick[:, n:n + 1], zero[:], zero[:], ALU.add)

            def image(b, m):
                def turn_q(i):
                    pool.wait_ge(qk_lo, b * UNITS + i + 1)
                    if i == 0:
                        pool.wait_ge(stored[2][0], b * 64 + 16)
                    for a in range(2):
                        src = ap(q_parts[:, ROWS * P * i + W * a:ROWS * P * i + W * a + 1],
                                 [(P, ROWS), (HALF, 2), (1, HALF)]).bitcast(F32)
                        dst = ap(q_cols[m][:, 0, HALF * a + ROWS * i:HALF * a + ROWS * i + 1],
                                 [(1, ROWS), (64, 2), (P, HALF)])
                        last = pool.tensor_tensor(dst, src, ap(zero[:], [(0, ROWS), (0, 2), (0, HALF)]), ALU.add)
                    last.then_inc(q_turned, 1)

                def split_next(s):
                    if by_pool(s) and s < SPLITS + 2:
                        split_low(pool, b, m, s)

                for s in range(AHEAD):
                    split_next(s)
                for i in range(UNITS):
                    split_next(2 * i + AHEAD)
                    split_next(2 * i + AHEAD + 1)
                    if i >= TURN_LATE:
                        turn_q(i - TURN_LATE)
                for i in range(UNITS - TURN_LATE, UNITS):
                    turn_q(i)
                wait(amax_step, b * (UNITS + 1) + UNITS + 1, 0)
                pool.partition_all_reduce(amax_all[:], amax_p[:], P, RMAX).then_inc(amax_done, 1)
                for s in range(SPLITS + 2, ALL_SPLITS):
                    split_low(pool, b, m, s)
                for g in range(len(APPLY)):
                    if g == 0:
                        pool.wait_ge(lo_split_pool, (b + 1) * (ALL_SPLITS - DVE_SPLITS))
                    pool.wait_ge(pt_hi, b * len(APPLY) + g + 1)
                    pool.wait_ge(pt_out, b * len(APPLY) + g + 1)
                    for a in range(2):
                        half = slice(64 * a, 64 * a + 64)
                        high, low = (pt[half, g % 2, part, :, half] for part in range(2))
                        last = pool.tensor_tensor(low, whole(g)[half], high, ALU.subtract)
                    last.then_inc(pt_lo, 1)

            with pool.Fori(0, B, 2) as b:
                for m in range(2):
                    image(b + m, m)


_OUT = ((16, 512, 64, 64), "float32")


def kernel(x, L0_conv_Wq, L0_conv_bq, L0_conv_Wk, L0_conv_bk, L0_conv_Wv, L0_conv_bv, L0_conv_gamma):
    import numpy as np
    import concourse.bacc as bacc
    from concourse.bass_utils import run_bass_kernel_spmd

    nc = bacc.Bacc("TRN2", target_bir_lowering=False, num_devices=1)
    wq, wk, wv = (np.asarray(w) for w in (L0_conv_Wq, L0_conv_Wk, L0_conv_Wv))
    given = {
        "x": np.asarray(x),
        "wqk_t": np.concatenate([wq.T, wk.T], axis=1),
        "bqk": np.concatenate([np.asarray(L0_conv_bq), np.asarray(L0_conv_bk)]).reshape(-1, 1),
        "wv_t": wv.T,
        "wv": wv,
        "bv": np.asarray(L0_conv_bv).reshape(-1, 128).T,
        "gamma": np.broadcast_to(np.asarray(L0_conv_gamma).reshape(1, 1), (128, 1)),
    }
    arrays = {f"{name}_dram": np.ascontiguousarray(a) for name, a in given.items()}
    args = [nc.dram_tensor(name, a.shape, mybir.dt.from_np(a.dtype), kind="ExternalInput").ap()
            for name, a in arrays.items()]
    shape, dtype = _OUT
    args.append(nc.dram_tensor("out_dram", shape, mybir.dt.from_np(np.dtype(dtype)), kind="ExternalOutput").ap())
    criss_cross(nc, *args)
    return run_bass_kernel_spmd(nc, [arrays], core_ids=[0]).results[0]["out_dram"]
```
